# Optimizing a Trainium2 kernel written in Bass

```python
import numpy as np
import jax
import jax.numpy as jnp

def _softmax(x, axis=-1):
    return jax.nn.softmax(x, axis=axis)

def _gelu(x):
    return jax.nn.gelu(x, approximate=True)

def _silu(x):
    return jax.nn.silu(x)

def _sigmoid(x):
    return jax.nn.sigmoid(x)

def _layernorm(x, axis=-1, eps=1e-05):
    m = jnp.mean(x, axis=axis, keepdims=True)
    v = jnp.var(x, axis=axis, keepdims=True)
    return (x - m) / jnp.sqrt(v + eps)

def _scatter_add(tgt, idx, src, axis=0):
    return tgt.at[idx].add(src)

def _segment_sum(src, seg, n):
    return jax.ops.segment_sum(src, seg, n)
kernel_name = 'mk_prb_d1_jaxref_r8_94a32c'

def setup_inputs(seed: int=0):
    np.random.seed(seed)
    _w = jnp.asarray

    def _L0_attn_setup():
        import jax, jax.numpy as jnp
        import numpy as np
        D_MODEL, N_QUERY, N_HEAD = (128, 2, 8)
        D_HEAD = D_MODEL // (N_QUERY * N_HEAD)
        KV = D_HEAD * N_HEAD

        def _reference_tuple_inner(x, Wq, Wk, Wv, memory, memory_norm, memory_weight):
            B, S, _ = x.shape
            QH = N_QUERY * N_HEAD
            scale = 1.0 / jnp.sqrt(jnp.float32(D_HEAD))
            q = x @ Wq
            k = x @ Wk
            v = x @ Wv
            q4 = q.reshape(B, S, QH, D_HEAD)
            k4 = jnp.repeat(k.reshape(B, S, N_HEAD, D_HEAD), N_QUERY, axis=2)
            v4 = jnp.repeat(v.reshape(B, S, N_HEAD, D_HEAD), N_QUERY, axis=2)
            scores = jnp.einsum('bsnd,btnd->bnst', q4, k4) * scale
            probs = jax.nn.softmax(scores, axis=-1)
            a_dot = jnp.einsum('bnst,btnd->bsnd', probs, v4)
            sigma_q = jax.nn.elu(q.reshape(B, S, N_QUERY, KV))
            num = sigma_q @ memory
            den = (sigma_q @ memory_norm)[..., None]
            a_mem = (num / den).reshape(B, S, QH, D_HEAD)
            sigma_k = jax.nn.elu(k)
            retrieved = sigma_k @ memory / (sigma_k @ memory_norm)[..., None]
            new_memory = memory + jnp.einsum('bsk,bsv->kv', sigma_k, v - retrieved)
            new_memory_norm = memory_norm + jnp.sum(sigma_k, axis=(0, 1))
            w = jax.nn.sigmoid(memory_weight)
            out = (a_dot * (1.0 - w) + a_mem * w).reshape(B, S, D_MODEL)
            return (out, new_memory, new_memory_norm)
        key = jax.random.key(seed)
        ks = jax.random.split(key, 6)
        B, S = (2, 256)
        x = jax.random.normal(ks[0], (B, S, D_MODEL), jnp.float32)
        Wq = jax.random.normal(ks[1], (D_MODEL, D_MODEL), jnp.float32) / np.sqrt(D_MODEL)
        Wk = jax.random.normal(ks[2], (D_MODEL, KV), jnp.float32) / np.sqrt(D_MODEL)
        Wv = jax.random.normal(ks[3], (D_MODEL, KV), jnp.float32) / np.sqrt(D_MODEL)
        memory = jax.random.normal(ks[4], (KV, KV), jnp.float32)
        memory_norm = jnp.ones((KV,), jnp.float32)
        memory_weight = jnp.ones((1,), jnp.float32)
        return {'x': x, 'Wq': Wq, 'Wk': Wk, 'Wv': Wv, 'memory': memory, 'memory_norm': memory_norm, 'memory_weight': memory_weight}
    _L0_attn_in = _L0_attn_setup()

    def _L0_ffn_setup():
        import jax, jax.numpy as jnp
        import numpy as np
        E, TOPK, R = (8, 2, 16)
        D, H, GH = (128, 16, 32)
        HD = D // H
        SCALE = HD ** (-0.5)

        def _svd_moe(x, Wm, U, S, V, b, idx, gates):
            main = jnp.einsum('bsd,od->bso', x, Wm)
            Ug, Sg, Vg = (U[idx], S[idx], V[idx])
            xv = jnp.einsum('bsd,bkrd->bksr', x, Vg)
            xvs = xv * Sg[:, :, None, :]
            eo = jnp.einsum('bksr,bkor->bkso', xvs, Ug)
            expert = jnp.einsum('bkso,bk->bso', eo, gates)
            return main + expert + b
        key = jax.random.key(seed)
        ks = jax.random.split(key, 32)
        B, S = (32, 257)
        inp = {'hidden_states': jax.random.normal(ks[0], (B, S, D), jnp.float32)}
        inp['gw1'] = jax.random.normal(ks[1], (GH, D), jnp.float32) * 0.02
        inp['gb1'] = jnp.zeros((GH,), jnp.float32)
        inp['gw2'] = jax.random.normal(ks[2], (E, GH), jnp.float32) * 0.02
        inp['gb2'] = jnp.zeros((E,), jnp.float32)
        i = 3
        for p in ('q', 'k', 'v', 'o'):
            inp[p + 'Wm'] = jax.random.normal(ks[i], (D, D), jnp.float32) * 0.02
            i += 1
            inp[p + 'U'] = jax.random.normal(ks[i], (E, D, R), jnp.float32) * 0.02
            i += 1
            inp[p + 'S'] = jax.random.normal(ks[i], (E, R), jnp.float32) * 0.1
            i += 1
            inp[p + 'V'] = jax.random.normal(ks[i], (E, R, D), jnp.float32) * 0.02
            i += 1
            inp[p + 'b'] = jnp.zeros((D,), jnp.float32)
        return inp
    _L0_ffn_in = _L0_ffn_setup()
    _d = {'L0_attn_x': _L0_attn_in['x'], 'L0_attn_Wq': _L0_attn_in['Wq'], 'L0_attn_Wk': _L0_attn_in['Wk'], 'L0_attn_Wv': _L0_attn_in['Wv'], 'L0_attn_memory': _L0_attn_in['memory'], 'L0_attn_memory_norm': _L0_attn_in['memory_norm'], 'L0_attn_memory_weight': _L0_attn_in['memory_weight'], 'L0_ffn_gw1': _L0_ffn_in['gw1'], 'L0_ffn_gb1': _L0_ffn_in['gb1'], 'L0_ffn_gw2': _L0_ffn_in['gw2'], 'L0_ffn_gb2': _L0_ffn_in['gb2'], 'L0_ffn_qWm': _L0_ffn_in['qWm'], 'L0_ffn_qU': _L0_ffn_in['qU'], 'L0_ffn_qS': _L0_ffn_in['qS'], 'L0_ffn_qV': _L0_ffn_in['qV'], 'L0_ffn_qb': _L0_ffn_in['qb'], 'L0_ffn_kWm': _L0_ffn_in['kWm'], 'L0_ffn_kU': _L0_ffn_in['kU'], 'L0_ffn_kS': _L0_ffn_in['kS'], 'L0_ffn_kV': _L0_ffn_in['kV'], 'L0_ffn_kb': _L0_ffn_in['kb'], 'L0_ffn_vWm': _L0_ffn_in['vWm'], 'L0_ffn_vU': _L0_ffn_in['vU'], 'L0_ffn_vS': _L0_ffn_in['vS'], 'L0_ffn_vV': _L0_ffn_in['vV'], 'L0_ffn_vb': _L0_ffn_in['vb'], 'L0_ffn_oWm': _L0_ffn_in['oWm'], 'L0_ffn_oU': _L0_ffn_in['oU'], 'L0_ffn_oS': _L0_ffn_in['oS'], 'L0_ffn_oV': _L0_ffn_in['oV'], 'L0_ffn_ob': _L0_ffn_in['ob']}
    _x0 = _d['L0_attn_x']
    _d['L0_attn_x'] = jax.random.normal(jax.random.fold_in(jax.random.key(seed), 1), (4, 1024, 128), dtype=_x0.dtype)
    del _x0
    return _d

def reference(L0_attn_x, L0_attn_Wq, L0_attn_Wk, L0_attn_Wv, L0_attn_memory, L0_attn_memory_norm, L0_attn_memory_weight, L0_ffn_gw1, L0_ffn_gb1, L0_ffn_gw2, L0_ffn_gb2, L0_ffn_qWm, L0_ffn_qU, L0_ffn_qS, L0_ffn_qV, L0_ffn_qb, L0_ffn_kWm, L0_ffn_kU, L0_ffn_kS, L0_ffn_kV, L0_ffn_kb, L0_ffn_vWm, L0_ffn_vU, L0_ffn_vS, L0_ffn_vV, L0_ffn_vb, L0_ffn_oWm, L0_ffn_oU, L0_ffn_oS, L0_ffn_oV, L0_ffn_ob):

    def _L0_attn_ref(x, Wq, Wk, Wv, memory, memory_norm, memory_weight):
        import jax, jax.numpy as jnp
        import numpy as np
        D_MODEL, N_QUERY, N_HEAD = (128, 2, 8)
        D_HEAD = D_MODEL // (N_QUERY * N_HEAD)
        KV = D_HEAD * N_HEAD

        def _reference_tuple_inner(x, Wq, Wk, Wv, memory, memory_norm, memory_weight):
            B, S, _ = x.shape
            QH = N_QUERY * N_HEAD
            scale = 1.0 / jnp.sqrt(jnp.float32(D_HEAD))
            q = x @ Wq
            k = x @ Wk
            v = x @ Wv
            q4 = q.reshape(B, S, QH, D_HEAD)
            k4 = jnp.repeat(k.reshape(B, S, N_HEAD, D_HEAD), N_QUERY, axis=2)
            v4 = jnp.repeat(v.reshape(B, S, N_HEAD, D_HEAD), N_QUERY, axis=2)
            scores = jnp.einsum('bsnd,btnd->bnst', q4, k4) * scale
            probs = jax.nn.softmax(scores, axis=-1)
            a_dot = jnp.einsum('bnst,btnd->bsnd', probs, v4)
            sigma_q = jax.nn.elu(q.reshape(B, S, N_QUERY, KV))
            num = sigma_q @ memory
            den = (sigma_q @ memory_norm)[..., None]
            a_mem = (num / den).reshape(B, S, QH, D_HEAD)
            sigma_k = jax.nn.elu(k)
            retrieved = sigma_k @ memory / (sigma_k @ memory_norm)[..., None]
            new_memory = memory + jnp.einsum('bsk,bsv->kv', sigma_k, v - retrieved)
            new_memory_norm = memory_norm + jnp.sum(sigma_k, axis=(0, 1))
            w = jax.nn.sigmoid(memory_weight)
            out = (a_dot * (1.0 - w) + a_mem * w).reshape(B, S, D_MODEL)
            return (out, new_memory, new_memory_norm)
        return _reference_tuple_inner(x, Wq, Wk, Wv, memory, memory_norm, memory_weight)[0]

    def _L0_ffn_ref(hidden_states, gw1, gb1, gw2, gb2, qWm, qU, qS, qV, qb, kWm, kU, kS, kV, kb, vWm, vU, vS, vV, vb, oWm, oU, oS, oV, ob):
        import jax, jax.numpy as jnp
        import numpy as np
        E, TOPK, R = (8, 2, 16)
        D, H, GH = (128, 16, 32)
        HD = D // H
        SCALE = HD ** (-0.5)

        def _svd_moe(x, Wm, U, S, V, b, idx, gates):
            main = jnp.einsum('bsd,od->bso', x, Wm)
            Ug, Sg, Vg = (U[idx], S[idx], V[idx])
            xv = jnp.einsum('bsd,bkrd->bksr', x, Vg)
            xvs = xv * Sg[:, :, None, :]
            eo = jnp.einsum('bksr,bkor->bkso', xvs, Ug)
            expert = jnp.einsum('bkso,bk->bso', eo, gates)
            return main + expert + b
        B, S, _ = hidden_states.shape
        pooled = hidden_states.mean(axis=1)
        h = jax.nn.relu(pooled @ gw1.T + gb1)
        logits = h @ gw2.T + gb2
        top_vals, top_idx = jax.lax.top_k(logits, TOPK)
        gates = jax.nn.softmax(top_vals, axis=-1)
        q = _svd_moe(hidden_states, qWm, qU, qS, qV, qb, top_idx, gates) * SCALE
        k = _svd_moe(hidden_states, kWm, kU, kS, kV, kb, top_idx, gates)
        v = _svd_moe(hidden_states, vWm, vU, vS, vV, vb, top_idx, gates)

        def shp(t):
            return t.reshape(B, S, H, HD).transpose(0, 2, 1, 3)
        q, k, v = (shp(q), shp(k), shp(v))
        attn = jax.nn.softmax(jnp.einsum('bhsd,bhtd->bhst', q, k), axis=-1)
        ctx = jnp.einsum('bhst,bhtd->bhsd', attn, v)
        ctx = ctx.transpose(0, 2, 1, 3).reshape(B, S, D)
        out = _svd_moe(ctx, oWm, oU, oS, oV, ob, top_idx, gates)
        return out
    x = L0_attn_x
    xn = _layernorm(x, axis=-1)
    x = x + _L0_attn_ref(xn, L0_attn_Wq, L0_attn_Wk, L0_attn_Wv, L0_attn_memory, L0_attn_memory_norm, L0_attn_memory_weight) + _L0_ffn_ref(xn, L0_ffn_gw1, L0_ffn_gb1, L0_ffn_gw2, L0_ffn_gb2, L0_ffn_qWm, L0_ffn_qU, L0_ffn_qS, L0_ffn_qV, L0_ffn_qb, L0_ffn_kWm, L0_ffn_kU, L0_ffn_kS, L0_ffn_kV, L0_ffn_kb, L0_ffn_vWm, L0_ffn_vU, L0_ffn_vS, L0_ffn_vV, L0_ffn_vb, L0_ffn_oWm, L0_ffn_oU, L0_ffn_oS, L0_ffn_oV, L0_ffn_ob)
    return x

_drawn_inputs = setup_inputs


def setup_inputs(seed=0):
    import zlib

    import numpy as np

    out = dict(_drawn_inputs(seed))
    spreads = {'L0_attn_memory_norm': (1.0, 0.2),
     'L0_ffn_gb1': (0.0, 2.0),
     'L0_ffn_gb2': (0.0, 0.8),
     'L0_ffn_qb': (0.0, 2.0),
     'L0_ffn_kb': (0.0, 2.0),
     'L0_ffn_vb': (0.0, 2.0),
     'L0_ffn_ob': (0.0, 2.0)}
    factors = {'L0_attn_Wk': 64.0,
     'L0_attn_Wv': 64.0,
     'L0_ffn_gw1': 64.0,
     'L0_ffn_gw2': 64.0,
     'L0_ffn_qWm': 8.0,
     'L0_ffn_qU': 8.0,
     'L0_ffn_qS': 8.0,
     'L0_ffn_qV': 8.0,
     'L0_ffn_kWm': 8.0,
     'L0_ffn_kU': 8.0,
     'L0_ffn_kS': 8.0,
     'L0_ffn_kV': 8.0,
     'L0_ffn_vWm': 8.0,
     'L0_ffn_vU': 29.547,
     'L0_ffn_vS': 29.948,
     'L0_ffn_vV': 28.057,
     'L0_ffn_oWm': 8.0,
     'L0_ffn_oU': 23.422,
     'L0_ffn_oS': 22.661,
     'L0_ffn_oV': 25.323}
    for name, (base, spread) in spreads.items():
        noise = np.random.default_rng([zlib.crc32(name.encode()), seed]).standard_normal(out[name].shape)
        drawn = base * np.exp(spread * noise) if base else spread * noise
        out[name] = jnp.asarray(drawn.astype(out[name].dtype))
    for name, factor in factors.items():
        out[name] = (out[name] * factor).astype(out[name].dtype)
    return out
```

```python
import concourse.bass as bass
from concourse import mybir
from contextlib import ExitStack

FP32 = mybir.dt.float32
BF16 = mybir.dt.bfloat16
ALU = mybir.AluOpType
ACT = mybir.ActivationFunctionType
AX = mybir.AxisListType


def attention_mix_kernel(nc, x, w_attn, w_main, u_t, v_er, s_er, b_qkv, b_o, g_w1, g_b1, g_w2, g_b2,
                         mem_aug, mem_w, ident_in, before_in, out):
    B, S, D = x.shape
    E = g_w2.shape[1]
    GH = g_w1.shape[1]
    HD = 8
    NH = D // HD
    T = S // 128
    J = 4
    HG = NH // J
    NG = B * 2 * HG
    NU = 2 * NG
    HQ = S // 2
    ST = HQ // 128
    SCALE = float(HD) ** -0.5
    EPS = 1e-5
    PARTS = 3
    BLOCKS = 6
    KR = BLOCKS * HD
    Q_RUNS = [(0, 3, 0), (3, 2, 0), (5, 1, 0)]
    K_RUNS = [(0, 3, 0), (3, 2, 1), (5, 1, 2)]
    LOADS = 2 * (len(Q_RUNS) + len(K_RUNS))
    SHIFTS = 8
    WEIGHTS = 15

    q_parts = nc.dram_tensor("q_parts", (NG, J, PARTS, HD, S), BF16, kind="Internal").ap()
    k_parts = nc.dram_tensor("k_parts", (NG, J, PARTS, HD, S), BF16, kind="Internal").ap()

    ctx = ExitStack()
    with ctx:
        def sb(name, shape, dt=FP32, stack=ctx):
            return stack.enter_context(nc.sbuf_tensor(name, shape, dt))

        def sem(name):
            return ctx.enter_context(nc.semaphore(name))

        x_all = sb("x_all", [128, B * T, D])
        v_all = sb("v_all", [128, NG, T, J, HD + 1])
        wo_all = sb("wo_all", [128, B, D])
        w_a = sb("w_a", [128, 3, D])
        w_m = sb("w_m", [128, 4, D])
        u_sb = sb("u_sb", [128, 4, D])
        v_sb = sb("v_sb", [128, 4, D])
        s_sb = sb("s_sb", [128, 4])
        bias = sb("bias", [128, 3])
        ob_row = sb("ob_row", [128, D])
        gw1 = sb("gw1", [128, GH])
        gb1 = sb("gb1", [GH, 1])
        gw2 = sb("gw2", [GH, E])
        gb2 = sb("gb2", [B, E])
        mem_sb = sb("mem_sb", [128, 2 * (D // 2 + 1)])
        mw = sb("mw", [128, 4])
        ident = sb("ident", [128, 128])
        before = sb("before", [B, E, E])
        v_now = sb("v_now", [128, 2, T, J, 32])
        exp_q = sb("exp_q", [128, 2, 2, S], BF16)
        exp_k = sb("exp_k", [128, 2, J, S], BF16)
        max_q = sb("max_q", [128, 2, J, S], BF16)
        max_k = sb("max_k", [128, 2, 2, S], BF16)
        neg_max = sb("neg_max", [128, 2, 16])
        shift_hi = sb("shift_hi", [16, 2, 128], BF16)
        shift_lo = sb("shift_lo", [16, 2, 128], BF16)
        pv_sb = sb("pv_sb", [128, 2, HQ])
        sum_inv = sb("sum_inv", [128, 2, ST, J])

        psum = ctx.enter_context(nc.psum_tensor("psum", [128, 8 * 512], FP32))

        def bank(n, k=1):
            return psum[:, n * 512:(n + k) * 512]

        x_loaded = sem("x_loaded")
        w_loaded = sem("w_loaded")
        init_done = sem("init_done")
        ones_step = sem("ones_step")
        stats_done = sem("stats_done")
        var_ready = sem("var_ready")
        std_ready = sem("std_ready")
        rstd_step = sem("rstd_step")
        xn_ready = sem("xn_ready")
        xt_ready = sem("xt_ready")
        xt_evac = sem("xt_evac")
        gate_pe = sem("gate_pe")
        gate_dve = sem("gate_dve")
        gate_act = sem("gate_act")
        ug_scaled = sem("ug_scaled")
        ug_ready = sem("ug_ready")
        weff_mm = sem("weff_mm")
        w_ready = sem("w_ready")
        xnow_ready = sem("xnow_ready")
        proj_ready = sem("proj_ready")
        full_ready = sem("full_ready")
        rest_ready = sem("rest_ready")
        mid_ready = sem("mid_ready")
        lo_ready = sem("lo_ready")
        stored = sem("stored")
        neg_ready = sem("neg_ready")
        tanh_ready = sem("tanh_ready")
        elu_step = sem("elu_step")
        elu_ready = sem("elu_ready")
        v_mm = sem("v_mm")
        v_evac = sem("v_evac")
        mem_mm = sem("mem_mm")
        mem_step = sem("mem_step")
        amem_ready = sem("amem_ready")
        x_step = sem("x_step")
        max_loaded = sem("max_loaded")
        exp_loaded = sem("exp_loaded")
        shift_loaded = sem("shift_loaded")
        v_staged = sem("v_staged")
        scores_ready = sem("scores_ready")
        exp_done = sem("exp_done")
        pv_done = sem("pv_done")
        pv_evac = sem("pv_evac")
        ring_full = sem("ring_full")
        ring_free = sem("ring_free")
        hi_done = sem("hi_done")
        inv_done = sem("inv_done")
        ctx_gathered = sem("ctx_gathered")
        ct_ready = sem("ct_ready")
        ct_evac = sem("ct_evac")
        moe_ready = sem("moe_ready")
        mix_ready = sem("mix_ready")
        out_ready = sem("out_ready")
        out_stored = sem("out_stored")

        prep = ExitStack()
        xnt_all = sb("xnt_all", [128, B, S], stack=prep)
        xnt = sb("xnt", [128, S], stack=prep)
        xn = sb("xn", [128, T, D], stack=prep)
        bn_st = sb("bn_st", [128, B * T, 6], stack=prep)
        bn_mv = sb("bn_mv", [128, B * T, 2], stack=prep)
        rstd = sb("rstd", [128, 4, B * T], stack=prep)
        pooled = sb("pooled", [128, 2 * B], stack=prep)
        pooled_b = sb("pooled_b", [128, B], stack=prep)
        gate_h = sb("gate_h", [GH, B], stack=prep)
        logits = sb("logits", [B, E], stack=prep)
        gate_s = sb("gate_s", [B, 8], stack=prep)
        above = sb("above", [B, E, E], stack=prep)
        ties = sb("ties", [B, E, E], stack=prep)
        rank = sb("rank", [B, E], stack=prep)
        gate_e = sb("gate_e", [B, E], stack=prep)
        gates = sb("gates", [B, E], stack=prep)
        gate_rep = sb("gate_rep", [B, E, 128 // E], stack=prep)
        gate_er = sb("gate_er", [128, B], stack=prep)
        gs = sb("gs", [128, 4], stack=prep)
        ug = sb("ug", [128, 4, D], stack=prep)
        w_now = sb("w_now", [128, 4, D], stack=prep)
        full = sb("full", [128, 4, S], stack=prep)
        rest = sb("rest", [128, 2, S], stack=prep)
        part_hi = sb("part_hi", [128, 4, S], BF16, stack=prep)
        part_mid = sb("part_mid", [128, 4, S], BF16, stack=prep)
        part_lo = sb("part_lo", [128, 4, S], BF16, stack=prep)
        elu_a = sb("elu_a", [128, S], stack=prep)
        elu_t = pv_sb[:, :, :].rearrange("p h c -> p (h c)")
        elu_e = xn[:, :, :].rearrange("p t d -> p (t d)")
        a_mem = elu_t.rearrange("p (t a c) -> p t a c", t=T, a=2)
        mem_inv = sb("mem_inv", [128, 2, T, 2], stack=prep)
        prep.close()
        p_exp = sb("p_exp", [128, 2, J, HQ])
        ctx_all = sb("ctx_all", [128, NU, ST, J * HD])
        ctx_b = sb("ctx_b", [128, T, D])
        ctx_t = sb("ctx_t", [128, S])
        mixed = sb("mixed", [128, T, D])
        result = sb("result", [128, T, D])

        vm = bank(4, 4).rearrange("p (t n) -> p t n", t=T)

        LEAD = 2
        FIRST, LAST = -LEAD * T, NU * T
        PERIOD = 4 * T
        ROUNDS = (LAST - LEAD * T - T) // PERIOD
        LOOP_FROM = T
        LOOP_TO = LOOP_FROM + ROUNDS * PERIOD
        END = LAST + T

        def has_max(s):
            return 0 <= s // T + LEAD < NU

        def has_scores(s):
            return 0 <= s < LAST

        def has_pv(s):
            return 0 <= s - 1 < LAST

        def has_shift(s):
            return s % T == 2 and 0 <= s // T + 1 < NU

        def has_out(s):
            return s % T == 5 and 0 <= s // T - 1 < NU

        entry, entries_before, n = {}, {}, 0
        for s in range(FIRST, END):
            entries_before[s] = n
            for kind, here in (("shift", has_shift(s)), ("out", has_out(s)), ("max", has_max(s)),
                               ("max2", has_max(s))):
                if here:
                    entry[kind, s] = n
                    n += 1
        n_entries = n
        PER_ROUND = entries_before[LOOP_FROM + PERIOD] - entries_before[LOOP_FROM]

        def slot(e):
            return bank(2 + 2 * (e % 2), 2)

        def stream(eng, substep):
            for s in range(FIRST, LOOP_FROM):
                substep(s, lambda base, step: base)
            with eng.Fori(0, ROUNDS) as i:
                for s in range(LOOP_FROM, LOOP_FROM + PERIOD):
                    substep(s, lambda base, step: i * step + base)
            for s in range(LOOP_TO, END):
                substep(s, lambda base, step: base)

        def batch_rows(eng, body):
            body(0, False)
            with eng.Fori(1, B) as b:
                body(b, True)

        def groups(eng, step_of_group):
            step_of_group(0, lambda base, step: base)
            rounds = (NG - 3) // 2
            with eng.Fori(0, rounds) as i:
                for g in (1, 2):
                    step_of_group(g, lambda base, step: i * step + base)
            for g in range(1 + 2 * rounds, NG):
                step_of_group(g, lambda base, step: base)

        def load_operand(eng, dst, slot_no, parts, group, runs, done):
            for h in range(2):
                rows = parts[group].rearrange("(p h) c d s -> h (c d) p s", h=2)[h]
                for block, count, part in runs:
                    at = 64 * h + HD * block
                    cols = slice(h, J, 2) if dst.shape[2] == J else slice(0, 2)
                    eng.dma_start(dst[at:at + HD * count, slot_no, cols, :],
                                  rows[HD * part:HD * (part + count)]).then_inc(done, 16)

        block = ctx.enter_context(nc.Block())

        @block.sync
        def _(sp):
            for b in range(B):
                sp.dma_start(x_all[:, b * T:(b + 1) * T, :],
                             x[b].rearrange("(t p) d -> p t d", p=128)).then_inc(x_loaded, 16)

            def rows_1(b, later):
                for k in range(4):
                    sp.wait_ge(lo_ready, b * 4 + (k + 1))
                    for c, part in enumerate((part_hi, part_mid, part_lo)):
                        dst, at = ((q_parts, c), (k_parts, PARTS - 1 - c))[k % 2]
                        sp.dma_start(
                            dst[bass.ds(b * (2 * HG) + (k // 2) * HG, HG), :, at, :, :]
                            .rearrange("g j d s -> (g j) d s"), part[:, k, :]).then_inc(stored, 16)

            batch_rows(sp, rows_1)

            sp.wait_ge(stored, 16 * PARTS * 4 * B)

            sp.wait_ge(init_done, 6)
            for g in range(2):
                load_operand(sp, max_q, g, q_parts, g, Q_RUNS, max_loaded)
                load_operand(sp, max_k, g, k_parts, g, K_RUNS, max_loaded)
                if g == 0:
                    load_operand(sp, exp_q, 0, q_parts, 0, Q_RUNS, exp_loaded)
                    load_operand(sp, exp_k, 0, k_parts, 0, K_RUNS, exp_loaded)

            def place_shift(unit, g, at):
                s = (unit - 1) * T + 2
                sp.wait_ge(ring_free, at(entry["shift", s] + 1, PER_ROUND))
                half = unit % 2
                for c, src in enumerate((shift_hi, shift_lo)):
                    for h in range(2):
                        row = 64 * h + KR + c
                        for p in range(2):
                            first = (2 * h + p) * ST
                            sp.dma_start(exp_q[row:row + 1, g % 2, p, half * HQ:(half + 1) * HQ],
                                         src[first:first + ST, half, :]).then_inc(shift_loaded, 16)

            place_shift(0, 0, lambda base, step: base)

            def group(g, at):
                if g + 1 < NG:
                    sp.wait_ge(scores_ready, at(8 * T * g + 1, 16 * T))
                    load_operand(sp, exp_q, (g + 1) % 2, q_parts, at(g + 1, 2), Q_RUNS, exp_loaded)
                    load_operand(sp, exp_k, (g + 1) % 2, k_parts, at(g + 1, 2), K_RUNS, exp_loaded)
                if g + 2 < NG:
                    sp.wait_ge(ring_full, at(entries_before[2 * T * g] + 1, PER_ROUND))
                    load_operand(sp, max_q, g % 2, q_parts, at(g + 2, 2), Q_RUNS, max_loaded)
                    load_operand(sp, max_k, g % 2, k_parts, at(g + 2, 2), K_RUNS, max_loaded)
                place_shift(2 * g + 1, g, at)
                if g + 1 < NG:
                    place_shift(2 * g + 2, g + 1, at)

            groups(sp, group)

            def rows_2(b, later):
                sp.wait_ge(out_ready, b + 1)
                sp.dma_start(out[b].rearrange("(t p) d -> p t d", p=128), result[:, :, :]).then_inc(out_stored, 16)

            batch_rows(sp, rows_2)

            sp.wait_ge(out_stored, 16 * B)

        @block.gpsimd
        def _(pool):
            pool.memset(v_all[:, :, :, :, :], 1.0).then_inc(init_done, 1)
            pool.memset(v_now[:, :, :, :, :], 0.0).then_inc(init_done, 1)
            pool.memset(exp_q[:, :, :, :], 0.0).then_inc(init_done, 1)
            pool.memset(max_q[:, :, :, :], 0.0).then_inc(init_done, 1)
            pool.memset(max_k[:, :, :, :], 0.0).then_inc(init_done, 1)
            pool.wait_ge(w_loaded, 16 * WEIGHTS)

            def rows_3(b, later):
                pool.wait_ge(xt_evac, 2 * B)
                if later:
                    pool.wait_ge(v_mm, b)
                pool.tensor_copy(xnt[:, :], xnt_all[:, b, :]).then_inc(xnow_ready, 1)
                for k in range(4):
                    pool.wait_ge(mid_ready, b * 4 + (k + 1))
                    pool.tensor_tensor(part_lo[:, k, :], rest[:, k % 2, :], part_mid[:, k, :],
                                       ALU.subtract).then_inc(lo_ready, 1)
                am = a_mem[:, :, :, :].rearrange("p t a c -> p t (a c)")
                pool.wait_ge(amem_ready, b + 1)
                pool.tensor_tensor(am, am, ob_row[:, :].unsqueeze(1).to_broadcast([128, T, D]),
                                   ALU.add).then_inc(x_step, 1)
                here = x_all[:, bass.ds(b * T, T), :]
                pool.wait_ge(x_step, b * 2 + 1)
                pool.wait_ge(w_loaded, 16 * WEIGHTS)
                pool.tensor_tensor(here, here, am, ALU.add).then_inc(x_step, 1)

            batch_rows(pool, rows_3)

            def stage_v(g, at):
                pool.tensor_copy(v_now[:, g % 2, :, :, 0:HD + 1],
                                 v_all[:, at(g, 2), :, :, :]).then_inc(v_staged, 1)

            pool.wait_ge(v_evac, B)
            for g in range(2):
                stage_v(g, lambda base, step: base)
            with pool.Fori(0, (NG - 2) // 2) as i:
                for g in (2, 3):
                    pool.wait_ge(pv_done, i * (4 * T) + 2 * T * (g - 1))
                    stage_v(g, lambda base, step: i * step + base)

            def rows_4(b, later):
                pool.wait_ge(mix_ready, b + 1)
                pool.wait_ge(x_step, 2 * B)
                pool.tensor_tensor(mixed[:, :, :], mixed[:, :, :], x_all[:, bass.ds(b * T, T), :],
                                   ALU.add).then_inc(x_step, 1)

            batch_rows(pool, rows_4)

        @block.scalar
        def _(act):
            weights = [(w_a[:, :, :], w_attn), (w_m[:, :, :], w_main), (u_sb[:, :, :], u_t), (v_sb[:, :, :], v_er),
                     (s_sb[:, :], s_er), (bias[:, :], b_qkv), (gw1[:, :], g_w1), (gb1[:, :], g_b1),
                     (gw2[:, :], g_w2), (mem_sb[:, :], mem_aug), (ident[:, :], ident_in),
                     (before[:, :, :], before_in), (ob_row[:, :], b_o.partition_broadcast(128)),
                     (gb2[:, :], g_b2.partition_broadcast(B)), (mw[:, 0:1], mem_w.partition_broadcast(128))]
            for dst, src in weights:
                act.dma_start(dst, src).then_inc(w_loaded, 16)

            act.wait_ge(var_ready, 1)
            nc.scalar.activation(rstd[:, 1, :], rstd[:, 0, :], ACT.Sqrt).then_inc(std_ready, 1)

            def rows_5(b, later):
                for h in range(2):
                    act.wait_ge(xt_ready, b * 2 + (h + 1))
                    nc.scalar.activation(xnt_all[:, b, h * HQ:(h + 1) * HQ], bank(h), ACT.Identity,
                                         accum_out=pooled[:, bass.ds(b * 2 + h, 1)]).then_inc(xt_evac, 1)

            batch_rows(act, rows_5)

            act.wait_ge(gate_dve, 3)
            nc.scalar.activation(gate_e[:, :], logits[:, :], ACT.Exp, bias=gate_s[:, 0:1]).then_inc(gate_act, 1)
            act.wait_ge(w_loaded, 16 * WEIGHTS)
            nc.scalar.activation(mw[:, 1:2], mw[:, 0:1], ACT.Exp, scale=-1.0).then_inc(gate_act, 1)

            def rows_6(b, later):
                if later:
                    act.wait_ge(stored, b * (16 * PARTS * 4))
                if later:
                    act.wait_ge(elu_ready, b)
                if later:
                    act.wait_ge(rest_ready, b * 4)

                def evacuate(k):
                    act.wait_ge(proj_ready, b * 4 + (k + 1))
                    src = bank(2 * (k % 2), 2)
                    off = bias[:, k % 2:k % 2 + 1] if k >= 2 else 0.0
                    nc.scalar.activation(full[:, k, :], src, ACT.Identity, bias=off)
                    nc.scalar.activation(part_hi[:, k, :], src, ACT.Identity, bias=off).then_inc(full_ready, 1)

                evacuate(0)
                evacuate(1)
                act.wait_ge(full_ready, b * 4 + 1)
                if later:
                    act.wait_ge(mem_mm, b)
                nc.scalar.activation(elu_a[:, :], full[:, 0, :], ACT.Relu, scale=-1.0).then_inc(neg_ready, 1)
                if later:
                    act.wait_ge(x_step, b * 2)
                act.wait_ge(neg_ready, b + 1)
                nc.scalar.activation(elu_t, elu_a[:, :], ACT.Tanh, scale=-0.5)
                nc.scalar.activation(elu_e, elu_a[:, :], ACT.Exp, scale=-1.0).then_inc(tanh_ready, 1)
                evacuate(2)
                evacuate(3)
                act.wait_ge(v_mm, b + 1)
                act.wait_ge(init_done, 7)
                for branch in range(2):
                    for hg in range(HG):
                        src = vm[:, :, (1 - branch) * D + hg * J * HD:(1 - branch) * D + (hg + 1) * J * HD]
                        last = nc.scalar.activation(
                            v_all[:, b * (2 * HG) + (branch * HG + hg), :, :, 0:HD],
                            src.rearrange("p t (j d) -> p t j d", j=J), ACT.Identity)
                last.then_inc(v_evac, 1)

            batch_rows(act, rows_6)

            def substep(s, at):
                if has_scores(s):
                    if s >= 2:
                        act.wait_ge(pv_done, at(s - 1, PERIOD))
                    for m, j in enumerate((0, 2, 1, 3)):
                        n = J * s + m
                        act.wait_ge(scores_ready, at(n + 1, J * PERIOD))
                        nc.scalar.activation(p_exp[:, s % 2, j, :], bank(n % 2), ACT.Exp,
                                             scale=SCALE).then_inc(exp_done, 1)
                unit = s // T - 1
                if s % T == 0 and 0 <= unit < NU:
                    act.wait_ge(pv_done, at(s, PERIOD))
                    if unit >= 2:
                        act.wait_ge(ring_full, at(entry["out", (unit - 1) * T + 5] + 1, PER_ROUND))
                    nc.scalar.activation(pv_sb[:, unit % 2, :], bank(6 + unit % 2),
                                         ACT.Identity).then_inc(pv_evac, 1)

            stream(act, substep)

            act.wait_ge(ring_free, n_entries)
            def rows_7(b, later):
                if later:
                    act.wait_ge(ct_ready, b)
                for hg in range(HG):
                    last = nc.scalar.activation(
                        ctx_b[:, :, hg * J * HD:(hg + 1) * J * HD].rearrange("p (h t) c -> p h t c", h=2),
                        ctx_all[:, bass.ds(b * (4 * HG) + (2 * HG + 2 * hg), 2), :, :], ACT.Identity)
                last.then_inc(ctx_gathered, 1)
                act.wait_ge(ct_ready, b + 1)
                if later:
                    act.wait_ge(moe_ready, b)
                nc.scalar.activation(ctx_t[:, :], bank(0, 2), ACT.Identity, bias=bias[:, 2:3]).then_inc(ct_evac, 1)

            batch_rows(act, rows_7)

        @block.tensor
        def _(pe):
            pe.wait_ge(w_loaded, 16 * WEIGHTS)
            def rows_8(b, later):
                if later:
                    pe.wait_ge(xt_evac, b * 2)
                for h in range(2):
                    pe.wait_ge(xn_ready, b * 2 + (h + 1))
                    for t in range(ST):
                        last = nc.tensor.transpose(bank(h)[:, t * 128:(t + 1) * 128], xn[:, h * ST + t, :],
                                                   ident[:, :])
                    last.then_inc(xt_ready, 1)

            batch_rows(pe, rows_8)

            pe.wait_ge(gate_dve, 1)
            nc.tensor.matmul(bank(2)[0:GH, 0:B], gw1[:, :], pooled_b[:, :], start=True, stop=True).then_inc(gate_pe, 1)
            pe.wait_ge(gate_dve, 2)
            nc.tensor.matmul(bank(3)[0:B, 0:E], gate_h[:, :], gw2[:, :], start=True, stop=True).then_inc(gate_pe, 1)
            pe.wait_ge(gate_dve, 4)
            nc.tensor.matmul(bank(2)[:, 0:B], gate_rep[:, :, :].rearrange("b e r -> b (e r)"), ident[0:B, 0:B],
                             start=True, stop=True).then_inc(gate_pe, 1)
            pe.wait_ge(gate_dve, 5)

            def rows_9(b, later):
                pe.wait_ge(ug_ready, b + 1)
                if later:
                    pe.wait_ge(amem_ready, b)
                for w in range(4):
                    last = nc.tensor.matmul(bank(4)[:, w * D:(w + 1) * D], v_sb[:, w, :], ug[:, w, :],
                                            start=True, stop=True)
                last.then_inc(weff_mm, 1)

                pe.wait_ge(xnow_ready, b + 1)
                if later:
                    pe.wait_ge(full_ready, b * 4)

                def project(k, w):
                    if k >= 2:
                        pe.wait_ge(full_ready, b * 4 + (k - 1))
                    for h in range(2):
                        last = nc.tensor.matmul(bank(2 * (k % 2) + h), w, xnt[:, h * HQ:(h + 1) * HQ],
                                                start=True, stop=True)
                    last.then_inc(proj_ready, 1)

                project(0, w_a[:, 0, :])
                project(1, w_a[:, 1, :])
                pe.wait_ge(w_ready, b + 1)
                project(2, w_now[:, 0, :])
                project(3, w_now[:, 1, :])
                for t in range(T):
                    last = nc.tensor.matmul(vm[:, t, :], xnt[:, t * 128:(t + 1) * 128],
                                            w_now[:, 2:4, :].rearrange("p w o -> p (w o)"), start=True, stop=True)
                last.then_inc(v_mm, 1)
                pe.wait_ge(elu_ready, b + 1)
                pe.wait_ge(v_evac, b + 1)
                for t in range(T):
                    last = nc.tensor.matmul(vm[:, t, 0:mem_sb.shape[1]], elu_a[:, t * 128:(t + 1) * 128], mem_sb[:, :],
                                            start=True, stop=True)
                last.then_inc(mem_mm, 1)

            batch_rows(pe, rows_9)

            pe.wait_ge(amem_ready, B)
            pe.wait_ge(full_ready, 4 * B)

            def claim(e, at):
                if e >= 2:
                    pe.wait_ge(ring_free, at(e - 1, PER_ROUND))

            def substep(s, at):
                unit, kt = s // T, s % T
                if has_shift(s):
                    e = entry["shift", s]
                    claim(e, at)
                    pe.wait_ge(ring_free, at(entry["max2", unit * T - 1] + 1, PER_ROUND))
                    nc.tensor.matmul(slot(e)[0:16, 0:128], neg_max[:, (unit + 1) % 2, :], ident[:, :],
                                     start=True, stop=True).then_inc(ring_full, 1)
                if has_out(s):
                    e = entry["out", s]
                    claim(e, at)
                    pe.wait_ge(pv_evac, at(unit, 4))
                    for t in range(ST):
                        last = nc.tensor.transpose(slot(e)[:, t * 128:(t + 1) * 128],
                                                   pv_sb[:, (unit - 1) % 2, t * 128:(t + 1) * 128], ident[:, :])
                    last.then_inc(ring_full, 1)

                def max_half(h, c):
                    e = entry["max" if h else "max2", s]
                    mu = unit + LEAD
                    mg, half, p, t = mu // 2, mu % 2, kt // ST, kt % ST
                    if c == 0:
                        claim(e, at)
                        if mu % 2 == 0 and kt == 0 and h:
                            pe.wait_ge(max_loaded, at(16 * LOADS * max(mg + 1, 2), 32 * LOADS))
                    q0 = half * HQ + t * 128
                    mm = nc.tensor.matmul(slot(e)[:, c * HQ:(c + 1) * HQ],
                                          max_q[:, mg % 2, 2 * p + h, q0:q0 + 128],
                                          max_k[:, mg % 2, p, c * HQ:(c + 1) * HQ], start=True, stop=True)
                    if c == 1:
                        mm.then_inc(ring_full, 1)

                def scores(m, j):
                    n = J * s + m
                    if n >= 2:
                        pe.wait_ge(exp_done, at(n - 1, J * PERIOD))
                    g, half = unit // 2, unit % 2
                    if kt == 0 and m == 0:
                        if half == 0:
                            pe.wait_ge(exp_loaded, at(16 * LOADS * (g + 1), 32 * LOADS))
                        pe.wait_ge(shift_loaded, at(16 * SHIFTS * (unit + 1), 64 * SHIFTS))
                    nc.tensor.matmul(bank(n % 2), exp_k[:, g % 2, j, kt * 128:(kt + 1) * 128],
                                     exp_q[:, g % 2, j // 2, half * HQ:(half + 1) * HQ],
                                     start=True, stop=True).then_inc(scores_ready, 1)

                def pv():
                    q = s - 1
                    u, t = q // T, q % T
                    pe.wait_ge(exp_done, at(J * s, J * PERIOD))
                    if t == 0:
                        if u >= 2:
                            pe.wait_ge(pv_evac, at(u - 1, 4))
                        if u % 2 == 0:
                            pe.wait_ge(v_staged, at(u // 2 + 1, 2))
                    for j in range(J):
                        last = nc.tensor.matmul(bank(6 + u % 2)[32 * j:32 * j + 32, :],
                                                v_now[:, (u // 2) % 2, t, j, :], p_exp[:, q % 2, j, :],
                                                start=(t == 0), stop=(t == T - 1))
                    last.then_inc(pv_done, 1)

                if has_scores(s):
                    scores(0, 0)
                if has_max(s):
                    max_half(1, 0)
                if has_scores(s):
                    scores(1, 2)
                if has_max(s):
                    max_half(1, 1)
                if has_pv(s):
                    pv()
                if has_scores(s):
                    scores(2, 1)
                if has_max(s):
                    max_half(0, 0)
                if has_scores(s):
                    scores(3, 3)
                if has_max(s):
                    max_half(0, 1)

            stream(pe, substep)

            pe.wait_ge(ring_free, n_entries)
            pe.wait_ge(exp_done, J * LAST)
            def rows_10(b, later):
                pe.wait_ge(ctx_gathered, b + 1)
                if later:
                    pe.wait_ge(ct_evac, b)
                for t in range(T):
                    last = nc.tensor.transpose(bank(t // 4)[:, (t % 4) * 128:(t % 4 + 1) * 128], ctx_b[:, t, :],
                                               ident[:, :])
                last.then_inc(ct_ready, 1)
                pe.wait_ge(ct_evac, b + 1)
                if later:
                    pe.wait_ge(out_ready, b)
                for t in range(T):
                    last = nc.tensor.matmul(bank(2 + t // 4)[:, (t % 4) * 128:(t % 4 + 1) * 128],
                                            ctx_t[:, t * 128:(t + 1) * 128], wo_all[:, b, :], start=True, stop=True)
                last.then_inc(moe_ready, 1)

            batch_rows(pe, rows_10)

        @block.vector
        def _(dve):
            nc.vector.memset(exp_k[:, :, :, :], 0.0).then_inc(ones_step, 1)
            dve.wait_ge(ones_step, 1)
            for h in range(2):
                nc.vector.memset(exp_k[64 * h + 32:64 * h + 64, :, h:J:2, :], 1.0).then_inc(init_done, 1)
            dve.wait_ge(x_loaded, 16 * B)
            def rows_11(b, later):
                for t in range(T):
                    last = nc.vector.bn_stats(bn_st[:, b * T + t, :], x_all[:, b * T + t, :])
                last.then_inc(stats_done, 1)

            batch_rows(dve, rows_11)

            dve.wait_ge(stats_done, B)
            for t in range(B * T):
                last = nc.vector.bn_aggr(bn_mv[:, t, :], bn_st[:, t, :])
            last.then_inc(stats_done, 1)
            dve.wait_ge(stats_done, B + 1)
            nc.vector.tensor_scalar(rstd[:, 0, :], bn_mv[:, :, 1], EPS, None, ALU.add).then_inc(var_ready, 1)
            dve.wait_ge(std_ready, 1)
            nc.vector.reciprocal(rstd[:, 2, :], rstd[:, 1, :]).then_inc(rstd_step, 1)
            dve.wait_ge(rstd_step, 1)
            nc.vector.tensor_tensor(rstd[:, 3, :], rstd[:, 2, :], rstd[:, 2, :], ALU.mult).then_inc(rstd_step, 1)
            dve.wait_ge(rstd_step, 2)
            nc.vector.tensor_tensor(rstd[:, 1, :], rstd[:, 3, :], rstd[:, 0, :], ALU.mult).then_inc(rstd_step, 1)
            dve.wait_ge(rstd_step, 3)
            nc.vector.tensor_scalar(rstd[:, 3, :], rstd[:, 1, :], -0.5, 1.5, ALU.mult, ALU.add).then_inc(rstd_step, 1)
            dve.wait_ge(rstd_step, 4)
            nc.vector.tensor_tensor(rstd[:, 0, :], rstd[:, 2, :], rstd[:, 3, :], ALU.mult).then_inc(rstd_step, 1)
            dve.wait_ge(rstd_step, 5)
            def rows_12(b, later):
                if later:
                    dve.wait_ge(xt_ready, b * 2)
                for t in range(T):
                    last = nc.vector.tensor_scalar(xn[:, t, :], x_all[:, b * T + t, :], bn_mv[:, b * T + t, 0:1],
                                                   rstd[:, 0, bass.ds(b * T + t, 1)], ALU.subtract, ALU.mult)
                    if t % ST == ST - 1:
                        last.then_inc(xn_ready, 1)

            batch_rows(dve, rows_12)

            steps = [0]

            def link(ins):
                steps[0] += 1
                ins.then_inc(rstd_step, 1)
                dve.wait_ge(rstd_step, 5 + steps[0])

            dve.wait_ge(xt_evac, 2 * B)
            pool_v = pooled[:, :].rearrange("p (b h) -> p b h", h=2)
            link(nc.vector.tensor_tensor(pooled_b[:, :], pool_v[:, :, 0], pool_v[:, :, 1], ALU.add))
            nc.vector.tensor_scalar(pooled_b[:, :], pooled_b[:, :], 1.0 / S, None, ALU.mult).then_inc(gate_dve, 1)
            dve.wait_ge(w_loaded, 16 * WEIGHTS)
            dve.wait_ge(gate_pe, 1)
            nc.vector.tensor_scalar(gate_h[:, :], bank(2)[0:GH, 0:B], gb1[:, 0:1], 0.0, ALU.add,
                                    ALU.max).then_inc(gate_dve, 1)
            dve.wait_ge(gate_pe, 2)
            link(nc.vector.tensor_tensor(logits[:, :], bank(3)[0:B, 0:E], gb2[:, :], ALU.add))
            nc.vector.tensor_reduce(gate_s[:, 0:1], logits[:, :], AX.X, ALU.max, negate=True).then_inc(gate_dve, 1)
            other = logits[:, :].unsqueeze(1).to_broadcast([B, E, E])
            own = logits[:, :].unsqueeze(2).to_broadcast([B, E, E])
            link(nc.vector.tensor_tensor(above[:, :, :], other, own, ALU.is_gt))
            link(nc.vector.tensor_tensor(ties[:, :, :], other, own, ALU.is_equal))
            link(nc.vector.tensor_tensor(ties[:, :, :], ties[:, :, :], before[:, :, :], ALU.mult))
            link(nc.vector.tensor_tensor(above[:, :, :], above[:, :, :], ties[:, :, :], ALU.add))
            link(nc.vector.tensor_reduce(rank[:, :], above[:, :, :], AX.X, ALU.add))
            link(nc.vector.tensor_scalar(rank[:, :], rank[:, :], 2.0, None, ALU.is_lt))
            dve.wait_ge(gate_act, 1)
            link(nc.vector.tensor_tensor(gates[:, :], gate_e[:, :], rank[:, :], ALU.mult))
            link(nc.vector.tensor_reduce(gate_s[:, 1:2], gates[:, :], AX.X, ALU.add))
            link(nc.vector.reciprocal(gate_s[:, 2:3], gate_s[:, 1:2]))
            link(nc.vector.tensor_scalar(gates[:, :], gates[:, :], gate_s[:, 2:3], None, ALU.mult))
            nc.vector.tensor_copy(gate_rep[:, :, :], gates[:, :].unsqueeze(2).to_broadcast([B, E, 128 // E]))\
                .then_inc(gate_dve, 1)
            dve.wait_ge(gate_act, 2)
            link(nc.vector.tensor_scalar(mw[:, 1:2], mw[:, 1:2], 1.0, None, ALU.add))
            link(nc.vector.reciprocal(mw[:, 2:3], mw[:, 1:2]))
            link(nc.vector.tensor_scalar(mw[:, 3:4], mw[:, 2:3], -1.0, 1.0, ALU.mult, ALU.add))
            dve.wait_ge(gate_pe, 3)
            link(nc.vector.tensor_copy(gate_er[:, :], bank(2)[:, 0:B]))
            nc.vector.tensor_copy(w_now[:, 3, :], w_a[:, 2, :]).then_inc(gate_dve, 1)

            def rows_13(b, later):
                nc.vector.tensor_scalar(gs[:, :], s_sb[:, :], gate_er[:, bass.ds(b, 1)], None,
                                        ALU.mult).then_inc(ug_scaled, 1)
                dve.wait_ge(ug_scaled, b + 1)
                for w in range(4):
                    last = nc.vector.tensor_scalar(ug[:, w, :], u_sb[:, w, :], gs[:, w:w + 1], None, ALU.mult)
                last.then_inc(ug_ready, 1)
                dve.wait_ge(weff_mm, b + 1)
                if later:
                    dve.wait_ge(v_mm, b)
                nc.vector.tensor_tensor(wo_all[:, b, :], bank(4)[:, 3 * D:4 * D], w_m[:, 3, :], ALU.add)
                nc.vector.tensor_tensor(w_now[:, 0:3, :], bank(4)[:, 0:3 * D].rearrange("p (w o) -> p w o", w=3),
                                        w_m[:, 0:3, :], ALU.add).then_inc(w_ready, 1)

                def split(k):
                    dve.wait_ge(full_ready, b * 4 + (k + 1))
                    if k >= 2:
                        dve.wait_ge(lo_ready, b * 4 + (k - 1))
                    nc.vector.tensor_tensor(rest[:, k % 2, :], full[:, k, :], part_hi[:, k, :],
                                            ALU.subtract).then_inc(rest_ready, 1)
                    dve.wait_ge(rest_ready, b * 4 + (k + 1))
                    nc.vector.tensor_copy(part_mid[:, k, :], rest[:, k % 2, :]).then_inc(mid_ready, 1)

                if later:
                    dve.wait_ge(lo_ready, b * 4)
                if later:
                    dve.wait_ge(stored, b * (16 * PARTS * 4))
                split(0)
                split(1)
                dve.wait_ge(tanh_ready, b + 1)
                nc.vector.scalar_tensor_tensor(elu_t, elu_e, 1.0, elu_t, ALU.add,
                                               ALU.mult).then_inc(elu_step, 1)
                dve.wait_ge(elu_step, b + 1)
                nc.vector.scalar_tensor_tensor(elu_a[:, :], full[:, 0, :], 0.0, elu_t, ALU.max,
                                               ALU.add).then_inc(elu_ready, 1)
                split(2)
                split(3)
                dve.wait_ge(mem_mm, b + 1)
                if later:
                    dve.wait_ge(x_step, b * 2)
                num = vm[:, :, 0:mem_sb.shape[1]].rearrange("p t (a c) -> p t a c", a=2)
                nc.vector.reciprocal(mem_inv[:, 0, :, :], num[:, :, :, D // 2]).then_inc(mem_step, 1)
                dve.wait_ge(mem_step, b * 2 + 1)
                nc.vector.tensor_scalar(mem_inv[:, 1, :, :], mem_inv[:, 0, :, :], mw[:, 2:3], None,
                                        ALU.mult).then_inc(mem_step, 1)
                dve.wait_ge(mem_step, b * 2 + 2)
                nc.vector.tensor_tensor(a_mem[:, :, :, :], num[:, :, :, 0:D // 2],
                                        mem_inv[:, 1, :, :].unsqueeze(3).to_broadcast([128, T, 2, D // 2]),
                                        ALU.mult).then_inc(amem_ready, 1)

            batch_rows(dve, rows_13)

            dve.wait_ge(x_step, 2 * B)
            dve.wait_ge(stored, 16 * PARTS * 4 * B)

            def substep(s, at):
                unit = s // T
                if has_shift(s):
                    e, u = entry["shift", s], unit + 1
                    dve.wait_ge(ring_full, at(e + 1, PER_ROUND))
                    if u >= 2:
                        dve.wait_ge(shift_loaded, at(16 * SHIFTS * (u - 1), 64 * SHIFTS))
                    nc.vector.tensor_copy(shift_hi[:, u % 2, :], slot(e)[0:16, 0:128]).then_inc(hi_done, 1)
                    dve.wait_ge(hi_done, at(u + 1, 4))
                    nc.vector.tensor_tensor(shift_lo[:, u % 2, :], slot(e)[0:16, 0:128], shift_hi[:, u % 2, :],
                                            ALU.subtract).then_inc(ring_free, 1)
                if has_out(s):
                    e, u = entry["out", s], unit - 1
                    dve.wait_ge(ring_full, at(e + 1, PER_ROUND))
                    heads = slot(e)[:, 0:HQ].rearrange("p (t j c) -> p t j c", t=ST, j=J)
                    nc.vector.reciprocal(sum_inv[:, u % 2, :, :], heads[:, :, :, HD]).then_inc(inv_done, 1)
                    dve.wait_ge(inv_done, at(u + 1, 4))
                    nc.vector.tensor_tensor(
                        ctx_all[:, at(u, 4), :, :].rearrange("p t (j d) -> p t j d", j=J),
                        heads[:, :, :, 0:HD],
                        sum_inv[:, u % 2, :, :].unsqueeze(3).to_broadcast([128, ST, J, HD]),
                        ALU.mult).then_inc(ring_free, 1)
                if has_max(s):
                    for h, kind in ((1, "max"), (0, "max2")):
                        e = entry[kind, s]
                        col = 8 * h + s % T
                        dve.wait_ge(ring_full, at(e + 1, PER_ROUND))
                        nc.vector.tensor_reduce(neg_max[:, (unit + LEAD) % 2, col:col + 1], slot(e), AX.X, ALU.max,
                                                negate=True).then_inc(ring_free, 1)

            stream(dve, substep)

            dve.wait_ge(ring_free, n_entries)
            def rows_14(b, later):
                if later:
                    dve.wait_ge(out_ready, b)
                for hg in range(HG):
                    last = nc.vector.tensor_scalar(
                        mixed[:, :, hg * J * HD:(hg + 1) * J * HD].rearrange("p (h t) c -> p h t c", h=2),
                        ctx_all[:, bass.ds(b * (4 * HG) + 2 * hg, 2), :, :], mw[:, 3:4], None, ALU.mult)
                last.then_inc(mix_ready, 1)
                dve.wait_ge(moe_ready, b + 1)
                dve.wait_ge(x_step, b + (2 * B + 1))
                if later:
                    dve.wait_ge(out_stored, b * 16)
                nc.vector.tensor_tensor(result[:, :, :], bank(2, 2).rearrange("p (t d) -> p t d", t=T),
                                        mixed[:, :, :], ALU.add).then_inc(out_ready, 1)

            batch_rows(dve, rows_14)

def kernel(**inputs):
    import numpy as np
    import concourse.bacc as bacc
    from concourse.bass_utils import run_bass_kernel_spmd as run

    a = {k.replace("L0_", ""): np.ascontiguousarray(v) for k, v in inputs.items()}
    ws = ("q", "k", "v", "o")
    E, D, R = a["ffn_qU"].shape
    kv = a["attn_Wk"].shape[1]
    hd = 8

    def twice(w):
        return np.repeat(w.reshape(D, kv // hd, hd), 2, axis=1).reshape(D, D)

    mem = np.zeros((D, 2 * (kv + 1)), np.float32)
    for i in range(2):
        mem[i * kv:(i + 1) * kv, i * (kv + 1):i * (kv + 1) + kv] = a["attn_memory"]
        mem[i * kv:(i + 1) * kv, i * (kv + 1) + kv] = a["attn_memory_norm"]
    B = a["attn_x"].shape[0]
    arrays = {
        "x": a["attn_x"],
        "w_attn": np.stack([a["attn_Wq"], twice(a["attn_Wk"]), twice(a["attn_Wv"])], axis=1),
        "w_main": np.stack([a[f"ffn_{w}Wm"].T for w in ws], axis=1),
        "u_t": np.stack([a[f"ffn_{w}U"].transpose(0, 2, 1).reshape(E * R, D) for w in ws], axis=1),
        "v_er": np.stack([a[f"ffn_{w}V"].reshape(E * R, D) for w in ws], axis=1),
        "s_er": np.stack([a[f"ffn_{w}S"].reshape(E * R) for w in ws], axis=1),
        "b_qkv": np.stack([a[f"ffn_{w}b"] for w in ("q", "k", "v")], axis=1),
        "b_o": a["ffn_ob"],
        "g_w1": a["ffn_gw1"].T,
        "g_b1": a["ffn_gb1"].reshape(-1, 1),
        "g_w2": a["ffn_gw2"].T,
        "g_b2": a["ffn_gb2"],
        "mem_aug": mem,
        "mem_w": a["attn_memory_weight"],
        "ident_in": np.eye(128, dtype=np.float32),
        "before_in": np.ascontiguousarray(np.broadcast_to(np.tri(E, k=-1, dtype=np.float32), (B, E, E))),
    }
    nc = bacc.Bacc("TRN2", target_bir_lowering=False, num_devices=1)
    maps, args = {}, []
    for name, v in arrays.items():
        v = np.ascontiguousarray(v)
        maps[f"in_{name}"] = v
        args.append(nc.dram_tensor(f"in_{name}", v.shape, mybir.dt.from_np(v.dtype), kind="ExternalInput").ap())
    out = nc.dram_tensor("out_0", a["attn_x"].shape, mybir.dt.float32, kind="ExternalOutput").ap()
    attention_mix_kernel(nc, *args, out)
    r = run(nc, [maps], core_ids=[0])
    return r.results[0]["out_0"]
```

```python
import concourse.bass as bass
from concourse import mybir
from contextlib import ExitStack

FP32 = mybir.dt.float32
BF16 = mybir.dt.bfloat16
ALU = mybir.AluOpType
ACT = mybir.ActivationFunctionType
AX = mybir.AxisListType


def attention_mix_kernel(nc, x, w_attn, w_main, u_t, v_er, s_er, b_qkv, b_o, g_w1, g_b1, g_w2, g_b2,
                         mem_aug, mem_w, ident_in, before_in, out):
    B, S, D = x.shape
    E = g_w2.shape[1]
    GH = g_w1.shape[1]
    HD = 8
    NH = D // HD
    T = S // 128
    J = 4
    HG = NH // J
    RG = 2 * HG
    RU = 2 * RG
    NG = B * RG
    NU = 2 * NG
    HQ = S // 2
    ST = HQ // 128
    GC = J * HD
    MW = D // 2 + 1
    SCALE = float(HD) ** -0.5
    EPS = 1e-5
    PARTS = 3
    KR = 6 * HD
    Q_RUNS = [(0, 3, 0), (3, 2, 0), (5, 1, 0)]
    K_RUNS = [(0, 3, 0), (3, 2, 1), (5, 1, 2)]
    LOADS = 2 * (len(Q_RUNS) + len(K_RUNS))
    SHIFTS = 8
    JOB = 16 * PARTS

    q_parts = nc.dram_tensor("q_parts", (NG, J, PARTS, HD, S), BF16, kind="Internal").ap()
    k_parts = nc.dram_tensor("k_parts", (NG, J, PARTS, HD, S), BF16, kind="Internal").ap()

    ctx = ExitStack()
    with ctx:
        def sb(name, shape, dt=FP32):
            return ctx.enter_context(nc.sbuf_tensor(name, shape, dt))

        def sem(name):
            return ctx.enter_context(nc.semaphore(name))

        x_all = sb("x_all", [128, B * T, D])
        w_a = sb("w_a", [128, 3, D])
        w_m = sb("w_m", [128, 4, D])
        u_sb = sb("u_sb", [128, 4, D])
        v_sb = sb("v_sb", [128, 4, D])
        s_sb = sb("s_sb", [128, 4])
        bias = sb("bias", [128, 3])
        ob_row = sb("ob_row", [128, D])
        gw1 = sb("gw1", [128, GH])
        gb1 = sb("gb1", [GH, 1])
        gw2 = sb("gw2", [GH, E])
        gb2 = sb("gb2", [1, E])
        mem_sb = sb("mem_sb", [128, 2 * MW])
        mw = sb("mw", [128, 4])
        ident = sb("ident", [128, 128])
        before = sb("before", [1, E, E])

        bn_st = sb("bn_st", [128, B * T, 6])
        bn_mv = sb("bn_mv", [128, B * T, 2])
        rstd = sb("rstd", [128, 3, B * T])
        pass_on = sb("pass_on", [1, 1])
        half_power = sb("half_power", [128, B * T])
        xn = sb("xn", [128, T, D])
        xnt = sb("xnt", [128, S])
        pooled = sb("pooled", [128, 1])
        gate_h = sb("gate_h", [GH, 2 * GH])
        logits = sb("logits", [1, E])
        gate_s = sb("gate_s", [1, 4])
        above = sb("above", [1, E, E])
        ties = sb("ties", [1, E, E])
        rank = sb("rank", [1, E])
        gate_e = sb("gate_e", [1, E])
        gates = sb("gates", [1, E])
        gate_rep = sb("gate_rep", [1, E, 128 // E])
        gs = sb("gs", [128, 4])
        ug = sb("ug", [128, 4, D])
        w_now = sb("w_now", [128, 3, D])
        wo_all = sb("wo_all", [128, B, D])
        full = sb("full", [128, 4, S])
        rest = sb("rest", [128, S])
        part_hi = sb("part_hi", [128, 4, S], BF16)
        part_mid = sb("part_mid", [128, 2, S], BF16)
        part_lo = sb("part_lo", [128, 2, S], BF16)
        elu_a = sb("elu_a", [128, S])
        elu_t = sb("elu_t", [128, S])
        elu_e = sb("elu_e", [128, S])
        a_mem = elu_e[:, :].rearrange("p (t a c) -> p t a c", t=T, a=2)
        mem_inv = sb("mem_inv", [128, 2, ST, 2])
        v_all = sb("v_all", [128, 2 * RG, T, J, HD])

        v_now = sb("v_now", [128, 2, T, J, 32])
        exp_q = sb("exp_q", [128, 2, 2, S], BF16)
        exp_k = sb("exp_k", [128, 2, J, S], BF16)
        max_q = sb("max_q", [128, 2, J, S], BF16)
        max_k = sb("max_k", [128, 2, 2, S], BF16)
        neg_max = sb("neg_max", [128, 2, 16])
        shift_hi = sb("shift_hi", [16, 2, 128], BF16)
        shift_lo = sb("shift_lo", [16, 2, 128], BF16)
        p_exp = sb("p_exp", [128, 2, J, HQ])
        pv_sb = sb("pv_sb", [128, 2, HQ])
        sum_inv = sb("sum_inv", [128, 2, ST, J])
        ctx_all = sb("ctx_all", [128, 2 * RU, ST, GC])

        ctx_b = elu_t[:, :].rearrange("p (t d) -> p t d", t=T)
        ctx_t = xnt
        mixed = sb("mixed", [128, T, D])

        psum = ctx.enter_context(nc.psum_tensor("psum", [128, 8 * 512], FP32))

        def bank(n, k=1):
            return psum[:, n * 512:(n + k) * 512]

        slot_a, slot_b = bank(2, 2), bank(4, 2)

        x_first = sem("x_first")
        x_rest = sem("x_rest")
        w_first = sem("w_first")
        w_loaded = sem("w_loaded")
        init_step = sem("init_step")
        init_done = sem("init_done")
        ln_step = sem("ln_step")
        ln_done = sem("ln_done")
        ones_step = sem("ones_step")
        w_scaled = sem("w_scaled")
        pow_in = sem("pow_in")
        pow_out = sem("pow_out")
        xn_ready = sem("xn_ready")
        to_act = sem("to_act")
        act_took = sem("act_took")
        to_dve = sem("to_dve")
        dve_took = sem("dve_took")
        gate_step = sem("gate_step")
        gate_exp = sem("gate_exp")
        neg_ready = sem("neg_ready")
        tanh_ready = sem("tanh_ready")
        elu_step = sem("elu_step")
        elu_ready = sem("elu_ready")
        first_step = sem("first_step")
        first_split = sem("first_split")
        split_step = sem("split_step")
        first_stored = sem("first_stored")
        q_stored = sem("q_stored")
        k_stored = sem("k_stored")
        x_step = sem("x_step")
        max_loaded = sem("max_loaded")
        exp_loaded = sem("exp_loaded")
        shift_loaded = sem("shift_loaded")
        v_staged = sem("v_staged")
        scores_ready = sem("scores_ready")
        exp_done = sem("exp_done")
        pv_done = sem("pv_done")
        pv_evac = sem("pv_evac")
        ring_full = sem("ring_full")
        ring_free = sem("ring_free")
        maxima_turned = sem("maxima_turned")
        maxima_taken = sem("maxima_taken")
        heads_turned = sem("heads_turned")
        heads_taken = sem("heads_taken")
        hi_done = sem("hi_done")
        inv_done = sem("inv_done")
        ctx_gathered = sem("ctx_gathered")
        ct_ready = sem("ct_ready")
        ct_evac = sem("ct_evac")
        moe_ready = sem("moe_ready")
        mix_ready = sem("mix_ready")
        x_mixed = sem("x_mixed")
        out_ready = sem("out_ready")
        out_stored = sem("out_stored")
        last_stored = sem("last_stored")

        ACT_TAKES = 7
        DVE_TAKES = 6
        GATE_STEPS = 17

        LEAD = T + T // 2
        FIRST, LAST = -LEAD, NU * T
        PERIOD = 4 * T
        ROW = RU * T
        LOOP_FROM = T
        ROUNDS = (LAST - LEAD - LOOP_FROM) // PERIOD
        LOOP_TO = LOOP_FROM + ROUNDS * PERIOD
        END = LAST + T // 2
        RR = ROW // PERIOD
        PAUSE = RR // 2

        def has_max(s):
            return 0 <= s + LEAD < LAST

        def has_scores(s):
            return 0 <= s < LAST

        def has_pv(s):
            return 0 <= s - 1 < LAST

        def has_shift(s):
            return s % T == T // 2 and 0 <= s // T + 1 < NU

        def has_out(s):
            return s % T == 2 and 0 <= s // T - 1 < NU

        entry, entries_before, n = {}, {}, 0
        for s in range(FIRST, END):
            entries_before[s] = n
            for kind in ("max", "max2"):
                if has_max(s):
                    entry[kind, s] = n
                    n += 1
        n_entries = n
        PER_ROUND = entries_before[LOOP_FROM + PERIOD] - entries_before[LOOP_FROM]

        def pv_bank(unit):
            return bank(6 + unit % 2)

        def slot(e):
            return bank(2 + 2 * (e % 2), 2)

        def fixed(base, step):
            return base

        def stream(eng, substep, pause, output):
            def rounds(count, index):
                with eng.Fori(0, count) as i:
                    for s in range(LOOP_FROM, LOOP_FROM + PERIOD):
                        substep(s, lambda base, step: index(i) * step + base)

            for s in range(FIRST, LOOP_FROM):
                substep(s, fixed)
            pause(0, None, fixed)
            rounds(PAUSE, lambda i: i)
            pause(1, None, lambda base, step: PAUSE * step + base)
            with eng.Fori(1, B - 1) as b:
                rounds(RR, lambda i: b * RR + i + (PAUSE - RR))
                pause(b + 1, b - 1, lambda base, step: b * (RR * step) + (PAUSE * step + base))
            done = PAUSE + (B - 2) * RR
            rounds(ROUNDS - done, lambda i: i + done)
            output(B - 2)
            for s in range(LOOP_TO, END):
                substep(s, fixed)
            output(B - 1)

        def load_operand(eng, dst, slot_no, parts, group, runs, done):
            for h in range(2):
                rows = parts[group].rearrange("(p h) c d s -> h (c d) p s", h=2)[h]
                for block, count, part in runs:
                    at = 64 * h + HD * block
                    cols = slice(h, J, 2) if dst.shape[2] == J else slice(0, 2)
                    eng.dma_start(dst[at:at + HD * count, slot_no, cols, :],
                                  rows[HD * part:HD * (part + count)]).then_inc(done, 16)

        def store_parts(eng, k, b, done):
            for c, part in enumerate((part_hi[:, k, :], part_mid[:, k % 2, :], part_lo[:, k % 2, :])):
                dst, at = ((q_parts, c), (k_parts, PARTS - 1 - c))[k % 2]
                first = b * RG + (k // 2) * HG
                groups = slice(first, first + HG) if isinstance(b, int) else bass.ds(first, HG)
                eng.dma_start(dst[groups, :, at, :, :].rearrange("g j d s -> (g j) d s"), part).then_inc(done, 16)

        WEIGHTS = [(w_m[:, :, :], w_main), (u_sb[:, :, :], u_t), (v_sb[:, :, :], v_er), (s_sb[:, :], s_er),
                   (gw1[:, :], g_w1), (gb1[:, :], g_b1), (gw2[:, :], g_w2), (mem_sb[:, :], mem_aug),
                   (before[:, :, :], before_in), (ob_row[:, :], b_o.partition_broadcast(128)),
                   (gb2[:, :], g_b2), (mw[:, 0:1], mem_w.partition_broadcast(128)), (bias[:, :], b_qkv)]

        block = ctx.enter_context(nc.Block())

        @block.sync
        def _(sp):
            for b in range(B):
                sp.dma_start(x_all[:, b * T:(b + 1) * T, :],
                             x[b].rearrange("(t p) d -> p t d", p=128)).then_inc(x_rest if b else x_first, 16)

            for k in range(2):
                sp.wait_ge(first_split, k + 1)
                store_parts(sp, k, 0, first_stored)

            sp.wait_ge(first_stored, 2 * JOB)
            sp.wait_ge(init_done, 7)
            for g in range(2):
                load_operand(sp, max_q, g, q_parts, g, Q_RUNS, max_loaded)
                load_operand(sp, max_k, g, k_parts, g, K_RUNS, max_loaded)
                if g == 0:
                    load_operand(sp, exp_q, 0, q_parts, 0, Q_RUNS, exp_loaded)
                    load_operand(sp, exp_k, 0, k_parts, 0, K_RUNS, exp_loaded)

            def place_shift(unit, g, at):
                sp.wait_ge(maxima_taken, at(unit + 1, 8))
                half = unit % 2
                for c, src in enumerate((shift_hi, shift_lo)):
                    for h in range(2):
                        row = 64 * h + KR + c
                        for p in range(2):
                            first = (2 * h + p) * ST
                            sp.dma_start(exp_q[row:row + 1, g % 2, p, half * HQ:(half + 1) * HQ],
                                         src[first:first + ST, half, :]).then_inc(shift_loaded, 16)

            place_shift(0, 0, fixed)

            def group(g, at):
                if g + 1 < NG:
                    sp.wait_ge(scores_ready, at(8 * T * g + 1, 32 * T))
                    load_operand(sp, exp_q, (g + 1) % 2, q_parts, at(g + 1, 4), Q_RUNS, exp_loaded)
                    load_operand(sp, exp_k, (g + 1) % 2, k_parts, at(g + 1, 4), K_RUNS, exp_loaded)
                place_shift(2 * g + 1, g, at)
                if g + 2 < NG:
                    sp.wait_ge(ring_full, at(entry["max", 2 * T * (g + 1) - LEAD] + 1, 2 * PER_ROUND))
                    if (g + 2) % HG == 0:
                        sp.wait_ge(q_stored, at(JOB * ((g + 2) // HG), JOB))
                        sp.wait_ge(k_stored, at(JOB * ((g + 2) // HG), JOB))
                    load_operand(sp, max_q, g % 2, q_parts, at(g + 2, 4), Q_RUNS, max_loaded)
                    load_operand(sp, max_k, g % 2, k_parts, at(g + 2, 4), K_RUNS, max_loaded)
                if g + 1 < NG:
                    place_shift(2 * g + 2, g + 1, at)

            group(0, fixed)
            turns = (NG - 3) // HG
            with sp.Fori(0, turns) as i:
                for g in range(1, 1 + HG):
                    group(g, lambda base, step: i * step + base)
            for g in range(1 + turns * HG, NG):
                group(g, fixed)

            sp.wait_ge(out_ready, B)
            sp.dma_start(out[B - 1].rearrange("(t p) d -> p t d", p=128), mixed[:, :, :]).then_inc(last_stored, 16)
            sp.wait_ge(last_stored, 16)
            sp.wait_ge(out_stored, 16 * (B - 1))

        @block.gpsimd
        def _(pool):
            pool.memset(half_power[:, :], -0.5).then_inc(init_step, 1)
            pool.wait_ge(init_step, 1)
            for part in (slice(0, T), slice(T, B * T)):
                pool.wait_ge(pow_in, 2 if part.start else 1)
                pool.tensor_tensor(rstd[:, 0, part], rstd[:, 1, part], half_power[:, part],
                                   ALU.pow).then_inc(pow_out, 1)
                if part.start:
                    break
                pool.memset(gate_h[:, :], 0.0).then_inc(init_done, 1)
                pool.memset(max_q[:, :, :, :].bitcast(FP32), 0.0).then_inc(init_done, 1)
                pool.memset(max_k[:, :, :, :].bitcast(FP32), 0.0).then_inc(init_done, 1)
                pool.memset(exp_q[:, :, :, :].bitcast(FP32), 0.0).then_inc(init_done, 1)
                pool.memset(v_now[:, :, :, :, :], 0.0).then_inc(init_step, 1)
                pool.wait_ge(init_step, 2)
                pool.memset(v_now[:, :, :, :, HD:HD + 1], 1.0).then_inc(init_done, 1)

            def split(k, b):
                q_or_k = (q_stored, k_stored)[k % 2]
                pool.wait_ge(act_took, b * ACT_TAKES + (2, 3, 5, 6)[k])
                pool.tensor_tensor(rest[:, :], full[:, k, :], part_hi[:, k, :], ALU.subtract)
                if isinstance(b, int) and b == 0:
                    pool.wait_ge(first_stored, 2 * JOB)
                else:
                    pool.wait_ge(q_or_k, b * (2 * JOB) + (k // 2 - 1) * JOB)
                pool.tensor_tensor(part_mid[:, k % 2, :], full[:, k, :], part_hi[:, k, :],
                                   ALU.subtract).then_inc(split_step, 1)
                n = 2 * k - 3
                pool.wait_ge(split_step, b * 8 + n)
                pool.tensor_tensor(part_lo[:, k % 2, :], rest[:, :], part_mid[:, k % 2, :],
                                   ALU.subtract).then_inc(split_step, 1)
                pool.wait_ge(split_step, b * 8 + (n + 1))
                pool.tensor_tensor(pass_on[:, :], half_power[0:1, 0:1], half_power[0:1, 0:1], ALU.add)
                store_parts(pool, k, b, q_or_k)

            def add_memory(b):
                am = a_mem.rearrange("p t a c -> p t (a c)")
                pool.wait_ge(dve_took, b * DVE_TAKES + 5)
                pool.tensor_tensor(am, am, ob_row[:, :].unsqueeze(1).to_broadcast([128, T, D]),
                                   ALU.add).then_inc(x_step, 1)
                here = x_all[:, bass.ds(b * T, T), :]
                pool.wait_ge(x_step, b * 2 + 1)
                pool.wait_ge(w_loaded, 16 * len(WEIGHTS))
                pool.tensor_tensor(here, here, am, ALU.add).then_inc(x_step, 1)

            def mix(o):
                pool.wait_ge(mix_ready, o + 1)
                pool.wait_ge(x_step, o * 2 + 2)
                pool.wait_ge(w_loaded, 16 * len(WEIGHTS))
                pool.tensor_tensor(mixed[:, :, :], mixed[:, :, :], x_all[:, bass.ds(o * T, T), :],
                                   ALU.add).then_inc(x_mixed, 1)

            def store_out(o):
                pool.wait_ge(out_ready, o + 1)
                pool.tensor_tensor(pass_on[:, :], half_power[0:1, 0:1], half_power[0:1, 0:1], ALU.add)
                pool.dma_start(out[o].rearrange("(t p) d -> p t d", p=128), mixed[:, :, :]).then_inc(out_stored, 16)

            def pause(b, o, at):
                for k in range(4) if not (isinstance(b, int) and b == 0) else (2, 3):
                    split(k, b)
                    if k == 2 and o is not None:
                        mix(o)
                        store_out(o)
                add_memory(b)

            def output(o):
                mix(o)
                if o < B - 1:
                    store_out(o)

            stream(pool, lambda s, at: None, pause, output)

        @block.scalar
        def _(act):
            act.dma_start(ident[:, :], ident_in).then_inc(w_first, 16)
            act.dma_start(w_a[:, :, :], w_attn).then_inc(w_first, 16)
            for dst, src in WEIGHTS:
                act.dma_start(dst, src).then_inc(w_loaded, 16)
            act.wait_ge(w_loaded, 16 * len(WEIGHTS))
            nc.scalar.activation(mw[:, 1:2], mw[:, 0:1], ACT.Exp, scale=-1.0).then_inc(gate_exp, 1)

            def evacuate(k, b):
                act.wait_ge(to_act, b * ACT_TAKES + (2, 3, 5, 6)[k])
                src = (slot_b, slot_a, slot_a, slot_b)[k]
                off = bias[:, k % 2:k % 2 + 1] if k >= 2 else 0.0
                nc.scalar.activation(full[:, k, :], src, ACT.Identity, bias=off)
                nc.scalar.activation(part_hi[:, k, :], src, ACT.Identity, bias=off).then_inc(act_took, 1)

            def evacuate_v(branch, b):
                act.wait_ge(to_act, b * ACT_TAKES + (4, 7)[branch])
                src = (slot_b, slot_a)[branch].rearrange("p (t n) -> p t n", t=T)
                for hg in range(HG):
                    last = nc.scalar.activation(
                        v_all[:, (b % 2) * RG + (branch * HG + hg), :, :, :],
                        src[:, :, hg * GC:(hg + 1) * GC].rearrange("p t (j d) -> p t j d", j=J), ACT.Identity)
                last.then_inc(act_took, 1)

            def prepare_a(b):
                act.wait_ge(to_act, b * ACT_TAKES + 1)
                nc.scalar.activation(xnt[:, :], slot_a, ACT.Identity, accum_out=pooled[:, :]).then_inc(act_took, 1)
                if not isinstance(b, int) or b:
                    act.wait_ge(q_stored, b * (2 * JOB) - JOB)
                    act.wait_ge(k_stored, b * (2 * JOB) - JOB)
                    act.wait_ge(elu_ready, b)
                evacuate(0, b)
                evacuate(1, b)
                act.wait_ge(act_took, b * ACT_TAKES + 2)
                nc.scalar.activation(elu_a[:, :], full[:, 0, :], ACT.Relu, scale=-1.0).then_inc(neg_ready, 1)
                if not isinstance(b, int) or b:
                    act.wait_ge(x_step, b * 2)
                act.wait_ge(neg_ready, b + 1)
                nc.scalar.activation(elu_t[:, :], elu_a[:, :], ACT.Tanh, scale=-0.5)
                nc.scalar.activation(elu_e[:, :], elu_a[:, :], ACT.Exp, scale=-1.0).then_inc(tanh_ready, 1)
                evacuate_v(0, b)

            def prepare_b(b):
                act.wait_ge(gate_step, b * GATE_STEPS + 2)
                nc.scalar.activation(gate_e[:, :], logits[:, :], ACT.Exp, bias=gate_s[:, 0:1]).then_inc(gate_exp, 1)
                evacuate(2, b)
                evacuate(3, b)
                evacuate_v(1, b)

            def stage_v(g, at):
                nc.scalar.activation(v_now[:, g % 2, :, :, 0:HD], v_all[:, at(g, 2) % (2 * RG), :, :, :],
                                     ACT.Identity).then_inc(v_staged, 1)

            def output(o):
                act.wait_ge(heads_taken, (o + 1) * RU)
                gather(o)

            def gather(o):
                for hg in range(HG):
                    last = nc.scalar.activation(
                        ctx_b[:, :, hg * GC:(hg + 1) * GC].rearrange("p (h t) c -> p h t c", h=2),
                        ctx_all[:, bass.ds((o % 2) * RU + (RU // 2 + 2 * hg), 2), :, :], ACT.Identity)
                last.then_inc(ctx_gathered, 1)
                act.wait_ge(ct_ready, o + 1)
                nc.scalar.activation(ctx_t[:, :], slot_b, ACT.Identity, bias=bias[:, 2:3]).then_inc(ct_evac, 1)

            def pause(b, o, at):
                if not (isinstance(b, int) and b == 0):
                    prepare_a(b)
                prepare_b(b)
                if o is not None:
                    act.wait_ge(elu_ready, b + 1)
                    gather(o)

            def substep(s, at):
                unit = s // T - 1
                if has_scores(s):
                    if s >= 2:
                        act.wait_ge(pv_done, at(s - 1, PERIOD))
                    for j in range(J):
                        n = J * s + j
                        act.wait_ge(scores_ready, at(n + 1, J * PERIOD))
                        nc.scalar.activation(p_exp[:, s % 2, j, :], bank(n % 2), ACT.Exp,
                                             scale=SCALE).then_inc(exp_done, 1)
                if s % T == 0 and 0 <= unit < NU:
                    act.wait_ge(pv_done, at(s, PERIOD))
                    nc.scalar.activation(pv_sb[:, unit % 2, :], bank(6 + unit % 2),
                                         ACT.Identity).then_inc(pv_evac, 1)
                if s % (2 * T) == 0 and 0 <= s < LAST - 2 * T:
                    stage_v(s // (2 * T) + 1, at)

            prepare_a(0)
            act.wait_ge(act_took, 4)
            act.wait_ge(init_done, 7)
            stage_v(0, fixed)
            stream(act, substep, pause, output)

        @block.tensor
        def _(pe):
            def project(w, dst):
                for h in range(2):
                    last = nc.tensor.matmul(dst[:, h * HQ:(h + 1) * HQ], w, xnt[:, h * HQ:(h + 1) * HQ],
                                            start=True, stop=True)
                last.then_inc(to_act, 1)

            def project_v(w, dst):
                for t in range(T):
                    last = nc.tensor.matmul(dst[:, t * D:(t + 1) * D], xnt[:, t * 128:(t + 1) * 128], w,
                                            start=True, stop=True)
                last.then_inc(to_act, 1)

            def prepare_a(b):
                pe.wait_ge(xn_ready, b + 1)
                for t in range(T):
                    last = nc.tensor.transpose(slot_a[:, t * 128:(t + 1) * 128], xn[:, t, :], ident[:, :])
                last.then_inc(to_act, 1)
                pe.wait_ge(act_took, b * ACT_TAKES + 1)
                project(w_a[:, 0, :], slot_b)
                project(w_a[:, 1, :], slot_a)
                pe.wait_ge(act_took, b * ACT_TAKES + 2)
                project_v(w_a[:, 2, :], slot_b)

            def read_memory(half, b):
                for t in range(ST):
                    last = nc.tensor.matmul(slot_b[:, 256 * t:256 * t + 2 * MW],
                                            elu_a[:, (half * ST + t) * 128:(half * ST + t + 1) * 128], mem_sb[:, :],
                                            start=True, stop=True)
                last.then_inc(to_dve, 1)

            def prepare_b(b):
                pe.wait_ge(act_took, b * ACT_TAKES + 3)
                if isinstance(b, int) and b == 0:
                    pe.wait_ge(w_loaded, 16 * len(WEIGHTS))
                    pe.wait_ge(w_scaled, 1)
                nc.tensor.matmul(slot_a[0:GH, 0:1], gw1[:, :], pooled[:, :], start=True, stop=True).then_inc(to_dve, 1)
                pe.wait_ge(dve_took, b * DVE_TAKES + 1)
                nc.tensor.matmul(slot_a[0:2 * GH, 64:64 + E], gate_h[:, :], gw2[:, :],
                                 start=True, stop=True).then_inc(to_dve, 1)
                pe.wait_ge(elu_ready, b + 1)
                pe.wait_ge(act_took, b * ACT_TAKES + 4)
                read_memory(0, b)
                pe.wait_ge(dve_took, b * DVE_TAKES + 2)
                nc.tensor.matmul(slot_a[:, 128:129], gate_rep[:, :, :].rearrange("b e r -> b (e r)"),
                                 ident[0:1, 0:1], start=True, stop=True).then_inc(to_dve, 1)
                pe.wait_ge(dve_took, b * DVE_TAKES + 3)
                read_memory(1, b)
                pe.wait_ge(dve_took, b * DVE_TAKES + 4)
                for w in range(4):
                    last = nc.tensor.matmul(slot_a[:, HQ + w * D:HQ + (w + 1) * D], v_sb[:, w, :], ug[:, w, :],
                                            start=True, stop=True)
                last.then_inc(to_dve, 1)
                pe.wait_ge(dve_took, b * DVE_TAKES + 6)
                project(w_now[:, 0, :], slot_a)
                project(w_now[:, 1, :], slot_b)
                pe.wait_ge(act_took, b * ACT_TAKES + 5)
                project_v(w_now[:, 2, :], slot_a)
                pe.wait_ge(act_took, b * ACT_TAKES + 6)

            def finish_row(o):
                pe.wait_ge(ctx_gathered, o + 1)
                for t in range(T):
                    last = nc.tensor.transpose(slot_b[:, t * 128:(t + 1) * 128], ctx_b[:, t, :], ident[:, :])
                last.then_inc(ct_ready, 1)
                pe.wait_ge(ct_evac, o + 1)
                for t in range(T):
                    last = nc.tensor.matmul(slot_a[:, t * 128:(t + 1) * 128], ctx_t[:, t * 128:(t + 1) * 128],
                                            wo_all[:, o, :], start=True, stop=True)
                last.then_inc(moe_ready, 1)
                pe.wait_ge(out_ready, o + 1)

            def pause(b, o, at):
                pe.wait_ge(ring_free, at(entries_before[LOOP_FROM], PER_ROUND))
                if not (isinstance(b, int) and b == 0):
                    prepare_a(b)
                prepare_b(b)
                pe.wait_ge(act_took, b * ACT_TAKES + 7)
                if o is not None:
                    finish_row(o)

            def output(o):
                if o < B - 1:
                    pe.wait_ge(ring_free, entries_before[LOOP_TO])
                finish_row(o)

            def claim(e, at):
                if e >= 2:
                    pe.wait_ge(ring_free, at(e - 1, PER_ROUND))

            def substep(s, at):
                unit, kt = s // T, s % T
                if has_out(s):
                    pe.wait_ge(pv_evac, at(unit, 4))
                    for t in range(ST):
                        last = nc.tensor.transpose(pv_bank(unit - 1)[:, t * 128:(t + 1) * 128],
                                                   pv_sb[:, (unit - 1) % 2, t * 128:(t + 1) * 128], ident[:, :])
                    last.then_inc(heads_turned, 1)

                def turn_maxima():
                    last_max = entry["max2", (unit + 2) * T - 1 - LEAD]
                    if unit >= 1:
                        pe.wait_ge(heads_taken, at(unit, 4))
                    pe.wait_ge(ring_free, at(last_max + 1, PER_ROUND))
                    nc.tensor.matmul(pv_bank(unit + 1)[0:16, 0:128], neg_max[:, (unit + 1) % 2, :], ident[:, :],
                                     start=True, stop=True).then_inc(maxima_turned, 1)

                def scores(j):
                    n = J * s + j
                    if n >= 2:
                        pe.wait_ge(exp_done, at(n - 1, J * PERIOD))
                    g, half = unit // 2, unit % 2
                    if kt == 0 and j == 0:
                        if half == 0:
                            pe.wait_ge(exp_loaded, at(16 * LOADS * (g + 1), 32 * LOADS))
                        pe.wait_ge(shift_loaded, at(16 * SHIFTS * (unit + 1), 64 * SHIFTS))
                    nc.tensor.matmul(bank(n % 2), exp_k[:, g % 2, j, kt * 128:(kt + 1) * 128],
                                     exp_q[:, g % 2, j // 2, half * HQ:(half + 1) * HQ],
                                     start=True, stop=True).then_inc(scores_ready, 1)

                def pv():
                    q = s - 1
                    u, t = q // T, q % T
                    pe.wait_ge(exp_done, at(J * s, J * PERIOD))
                    if t == 0 and u % 2 == 0:
                        pe.wait_ge(v_staged, at(u // 2 + 1, 2))
                    for j in range(J):
                        last = nc.tensor.matmul(bank(6 + u % 2)[32 * j:32 * j + 32, :],
                                                v_now[:, (u // 2) % 2, t, j, :], p_exp[:, q % 2, j, :],
                                                start=(t == 0), stop=(t == T - 1))
                    last.then_inc(pv_done, 1)

                def maxima(h, kind):
                    e = entry[kind, s]
                    mu, mt = (s + LEAD) // T, (s + LEAD) % T
                    mg, half, p, t = mu // 2, mu % 2, mt // ST, mt % ST
                    claim(e, at)
                    if half == 0 and mt == 0 and kind == "max":
                        pe.wait_ge(max_loaded, at(16 * LOADS * max(mg + 1, 2), 32 * LOADS))
                    q0 = half * HQ + t * 128
                    for c in range(2):
                        mm = nc.tensor.matmul(slot(e)[:, c * HQ:(c + 1) * HQ],
                                              max_q[:, mg % 2, 2 * p + h, q0:q0 + 128],
                                              max_k[:, mg % 2, p, c * HQ:(c + 1) * HQ], start=True, stop=True)
                    mm.then_inc(ring_full, 1)

                if has_scores(s):
                    scores(0)
                    scores(1)
                if has_pv(s):
                    pv()
                if has_scores(s):
                    scores(2)
                    scores(3)
                if has_max(s):
                    maxima(0, "max")
                if has_shift(s):
                    turn_maxima()
                if has_max(s):
                    maxima(1, "max2")

            pe.wait_ge(w_first, 32)
            prepare_a(0)
            pe.wait_ge(act_took, 4)
            stream(pe, substep, pause, output)

        @block.vector
        def _(dve):
            def statistics(part, k):
                for t in range(part.start, part.stop):
                    last = nc.vector.bn_stats(bn_st[:, t, :], x_all[:, t, :])
                last.then_inc(ln_step, 1)
                dve.wait_ge(ln_step, 5 * k + 1)
                for t in range(part.start, part.stop):
                    last = nc.vector.bn_aggr(bn_mv[:, t, :], bn_st[:, t, :])
                last.then_inc(ln_step, 1)
                dve.wait_ge(ln_step, 5 * k + 2)
                first, var, tmp = (rstd[:, i, part] for i in range(3))
                nc.vector.tensor_scalar(var, bn_mv[:, part, 1], EPS, None, ALU.add).then_inc(pow_in, 1)
                dve.wait_ge(pow_out, k + 1)
                nc.vector.tensor_tensor(tmp, first, first, ALU.mult).then_inc(ln_step, 1)
                dve.wait_ge(ln_step, 5 * k + 3)
                nc.vector.tensor_tensor(tmp, tmp, var, ALU.mult).then_inc(ln_step, 1)
                dve.wait_ge(ln_step, 5 * k + 4)
                nc.vector.tensor_scalar(tmp, tmp, -0.5, 1.5, ALU.mult, ALU.add).then_inc(ln_step, 1)
                dve.wait_ge(ln_step, 5 * k + 5)
                nc.vector.tensor_tensor(first, first, tmp, ALU.mult).then_inc(ln_done, 1)
                dve.wait_ge(ln_done, k + 1)

            def normalise(b):
                for t in range(T):
                    last = nc.vector.tensor_scalar(xn[:, t, :], x_all[:, b * T + t, :], bn_mv[:, b * T + t, 0:1],
                                                   rstd[:, 0, bass.ds(b * T + t, 1)], ALU.subtract, ALU.mult)
                last.then_inc(xn_ready, 1)

            dve.wait_ge(x_first, 16)
            statistics(slice(0, T), 0)
            normalise(0)
            nc.vector.memset(exp_k[:, :, :, :].bitcast(FP32), 0.0).then_inc(ones_step, 1)
            dve.wait_ge(ones_step, 1)
            for h in range(2):
                nc.vector.memset(exp_k[64 * h + 32:64 * h + 64, :, h:J:2, :], 1.0).then_inc(init_done, 1)
            first_rest = mixed[:, :, :].rearrange("p t d -> p (t d)")
            for k in range(2):
                dve.wait_ge(act_took, 2 + k)
                if k:
                    dve.wait_ge(first_split, 1)
                nc.vector.tensor_tensor(first_rest, full[:, k, :], part_hi[:, k, :],
                                        ALU.subtract).then_inc(first_step, 1)
                dve.wait_ge(first_step, 2 * k + 1)
                nc.vector.tensor_copy(part_mid[:, k, :], first_rest).then_inc(first_step, 1)
                dve.wait_ge(first_step, 2 * k + 2)
                nc.vector.tensor_tensor(part_lo[:, k, :], first_rest, part_mid[:, k, :],
                                        ALU.subtract).then_inc(first_split, 1)
            dve.wait_ge(x_rest, 16 * (B - 1))
            statistics(slice(T, B * T), 1)
            dve.wait_ge(w_loaded, 16 * len(WEIGHTS))
            nc.vector.tensor_scalar(gw1[:, :], gw1[:, :], 1.0 / S, None, ALU.mult).then_inc(w_scaled, 1)
            dve.wait_ge(gate_exp, 1)
            nc.vector.tensor_scalar(mw[:, 1:2], mw[:, 1:2], 1.0, None, ALU.add).then_inc(w_scaled, 1)
            dve.wait_ge(w_scaled, 2)
            nc.vector.reciprocal(mw[:, 2:3], mw[:, 1:2]).then_inc(w_scaled, 1)
            dve.wait_ge(w_scaled, 3)
            nc.vector.tensor_scalar(mw[:, 3:4], mw[:, 2:3], -1.0, 1.0, ALU.mult, ALU.add).then_inc(w_scaled, 1)
            dve.wait_ge(w_scaled, 4)

            def prepare_b(b):
                steps = [0]

                def link(ins):
                    steps[0] += 1
                    ins.then_inc(gate_step, 1)
                    dve.wait_ge(gate_step, b * GATE_STEPS + steps[0])

                dve.wait_ge(tanh_ready, b + 1)
                nc.vector.scalar_tensor_tensor(elu_t[:, :], elu_e[:, :], 1.0, elu_t[:, :], ALU.add,
                                               ALU.mult).then_inc(elu_step, 1)
                if isinstance(b, int) and b == 0:
                    dve.wait_ge(init_done, 7)
                dve.wait_ge(to_dve, b * DVE_TAKES + 1)
                nc.vector.tensor_scalar(gate_h[:, 0:1], slot_a[0:GH, 0:1], gb1[:, 0:1], 0.0, ALU.add,
                                        ALU.max).then_inc(dve_took, 1)
                dve.wait_ge(elu_step, b + 1)
                nc.vector.scalar_tensor_tensor(elu_a[:, :], full[:, 0, :], 0.0, elu_t[:, :], ALU.max,
                                               ALU.add).then_inc(elu_ready, 1)
                dve.wait_ge(to_dve, b * DVE_TAKES + 2)
                link(nc.vector.tensor_tensor(logits[:, :], slot_a[0:1, 64:64 + E], gb2[:, :], ALU.add))
                link(nc.vector.tensor_reduce(gate_s[:, 0:1], logits[:, :], AX.X, ALU.max, negate=True))
                other = logits[:, :].unsqueeze(1).to_broadcast([1, E, E])
                own = logits[:, :].unsqueeze(2).to_broadcast([1, E, E])
                link(nc.vector.tensor_tensor(above[:, :, :], other, own, ALU.is_gt))
                link(nc.vector.tensor_tensor(ties[:, :, :], other, own, ALU.is_equal))
                link(nc.vector.tensor_tensor(ties[:, :, :], ties[:, :, :], before[:, :, :], ALU.mult))
                link(nc.vector.tensor_tensor(above[:, :, :], above[:, :, :], ties[:, :, :], ALU.add))
                link(nc.vector.tensor_reduce(rank[:, :], above[:, :, :], AX.X, ALU.add))
                link(nc.vector.tensor_scalar(rank[:, :], rank[:, :], 2.0, None, ALU.is_lt))
                dve.wait_ge(gate_exp, b + 2)
                link(nc.vector.tensor_tensor(gates[:, :], gate_e[:, :], rank[:, :], ALU.mult))
                link(nc.vector.tensor_reduce(gate_s[:, 1:2], gates[:, :], AX.X, ALU.add))
                link(nc.vector.reciprocal(gate_s[:, 2:3], gate_s[:, 1:2]))
                link(nc.vector.tensor_scalar(gates[:, :], gates[:, :], gate_s[:, 2:3], None, ALU.mult))
                nc.vector.tensor_copy(gate_rep[:, :, :], gates[:, :].unsqueeze(2).to_broadcast([1, E, 128 // E]))\
                    .then_inc(dve_took, 1)

                def memory(half):
                    dve.wait_ge(to_dve, b * DVE_TAKES + (3, 5)[half])
                    num = slot_b.rearrange("p (t n) -> p t n", t=ST)[:, :, 0:2 * MW].rearrange(
                        "p t (a c) -> p t a c", a=2)
                    link(nc.vector.reciprocal(mem_inv[:, 0, :, :], num[:, :, :, MW - 1]))
                    link(nc.vector.tensor_scalar(mem_inv[:, 1, :, :], mem_inv[:, 0, :, :], mw[:, 2:3], None, ALU.mult))
                    nc.vector.tensor_tensor(a_mem[:, half * ST:(half + 1) * ST, :, :], num[:, :, :, 0:MW - 1],
                                            mem_inv[:, 1, :, :].unsqueeze(3).to_broadcast([128, ST, 2, MW - 1]),
                                            ALU.mult).then_inc(dve_took, 1)

                memory(0)
                dve.wait_ge(to_dve, b * DVE_TAKES + 4)
                link(nc.vector.tensor_scalar(gs[:, :], s_sb[:, :], slot_a[:, 128:129], None, ALU.mult))
                for w in range(4):
                    last = nc.vector.tensor_scalar(ug[:, w, :], u_sb[:, w, :], gs[:, w:w + 1], None, ALU.mult)
                last.then_inc(dve_took, 1)
                memory(1)
                dve.wait_ge(to_dve, b * DVE_TAKES + 6)
                nc.vector.tensor_tensor(wo_all[:, b, :], slot_a[:, HQ + 3 * D:HQ + 4 * D], w_m[:, 3, :], ALU.add)
                nc.vector.tensor_tensor(w_now[:, :, :], slot_a[:, HQ:HQ + 3 * D].rearrange("p (w o) -> p w o", w=3),
                                        w_m[:, 0:3, :], ALU.add).then_inc(dve_took, 1)
                assert steps[0] == GATE_STEPS

            def finish_row(o):
                if not isinstance(o, int) or o:
                    dve.wait_ge(out_stored, o * 16)
                for hg in range(HG):
                    last = nc.vector.tensor_scalar(
                        mixed[:, :, hg * GC:(hg + 1) * GC].rearrange("p (h t) c -> p h t c", h=2),
                        ctx_all[:, bass.ds((o % 2) * RU + 2 * hg, 2), :, :], mw[:, 3:4], None, ALU.mult)
                last.then_inc(mix_ready, 1)
                dve.wait_ge(x_mixed, o + 1)
                dve.wait_ge(moe_ready, o + 1)
                nc.vector.tensor_tensor(mixed[:, :, :], slot_a.rearrange("p (t d) -> p t d", t=T), mixed[:, :, :],
                                        ALU.add).then_inc(out_ready, 1)

            def pause(b, o, at):
                if not (isinstance(b, int) and b == 0):
                    normalise(b)
                prepare_b(b)
                if o is not None:
                    finish_row(o)

            def substep(s, at):
                unit = s // T
                def maximum(h, kind):
                    e = entry[kind, s]
                    mu, mt = (s + LEAD) // T, (s + LEAD) % T
                    col = 8 * h + mt
                    dve.wait_ge(ring_full, at(e + 1, PER_ROUND))
                    nc.vector.tensor_reduce(neg_max[:, mu % 2, col:col + 1], slot(e), AX.X, ALU.max,
                                            negate=True).then_inc(ring_free, 1)

                if has_out(s):
                    heads = pv_bank(unit - 1).rearrange("p (t j c) -> p t j c", t=ST, j=J)
                    dve.wait_ge(heads_turned, at(unit, 4))
                    nc.vector.reciprocal(sum_inv[:, (unit - 1) % 2, :, :], heads[:, :, :, HD]).then_inc(inv_done, 1)
                if has_max(s):
                    maximum(0, "max")
                if has_out(s):
                    dve.wait_ge(inv_done, at(unit, 4))
                    nc.vector.tensor_tensor(
                        ctx_all[:, at(unit - 1, 4) % (2 * RU), :, :].rearrange("p t (j d) -> p t j d", j=J),
                        heads[:, :, :, 0:HD],
                        sum_inv[:, (unit - 1) % 2, :, :].unsqueeze(3).to_broadcast([128, ST, J, HD]),
                        ALU.mult).then_inc(heads_taken, 1)
                if has_shift(s):
                    turned = pv_bank(unit + 1)[0:16, 0:128]
                    dve.wait_ge(maxima_turned, at(unit + 2, 4))
                    if unit >= 1:
                        dve.wait_ge(shift_loaded, at(16 * SHIFTS * unit, 64 * SHIFTS))
                    nc.vector.tensor_copy(shift_hi[:, (unit + 1) % 2, :], turned).then_inc(hi_done, 1)
                if has_max(s):
                    maximum(1, "max2")
                if has_shift(s):
                    dve.wait_ge(hi_done, at(unit + 2, 4))
                    nc.vector.tensor_tensor(shift_lo[:, (unit + 1) % 2, :], turned, shift_hi[:, (unit + 1) % 2, :],
                                            ALU.subtract).then_inc(maxima_taken, 1)

            stream(dve, substep, pause, finish_row)


def kernel(**inputs):
    import numpy as np
    import concourse.bacc as bacc
    from concourse.bass_utils import run_bass_kernel_spmd as run

    a = {k.replace("L0_", ""): np.ascontiguousarray(v) for k, v in inputs.items()}
    ws = ("q", "k", "v", "o")
    E, D, R = a["ffn_qU"].shape
    kv = a["attn_Wk"].shape[1]
    hd = 8

    def twice(w):
        return np.repeat(w.reshape(D, kv // hd, hd), 2, axis=1).reshape(D, D)

    mem = np.zeros((D, 2 * (kv + 1)), np.float32)
    for i in range(2):
        mem[i * kv:(i + 1) * kv, i * (kv + 1):i * (kv + 1) + kv] = a["attn_memory"]
        mem[i * kv:(i + 1) * kv, i * (kv + 1) + kv] = a["attn_memory_norm"]
    arrays = {
        "x": a["attn_x"],
        "w_attn": np.stack([a["attn_Wq"], twice(a["attn_Wk"]), twice(a["attn_Wv"])], axis=1),
        "w_main": np.stack([a[f"ffn_{w}Wm"].T for w in ws], axis=1),
        "u_t": np.stack([a[f"ffn_{w}U"].transpose(0, 2, 1).reshape(E * R, D) for w in ws], axis=1),
        "v_er": np.stack([a[f"ffn_{w}V"].reshape(E * R, D) for w in ws], axis=1),
        "s_er": np.stack([a[f"ffn_{w}S"].reshape(E * R) for w in ws], axis=1),
        "b_qkv": np.stack([a[f"ffn_{w}b"] for w in ("q", "k", "v")], axis=1),
        "b_o": a["ffn_ob"],
        "g_w1": a["ffn_gw1"].T,
        "g_b1": a["ffn_gb1"].reshape(-1, 1),
        "g_w2": a["ffn_gw2"].T,
        "g_b2": a["ffn_gb2"].reshape(1, E),
        "mem_aug": mem,
        "mem_w": a["attn_memory_weight"],
        "ident_in": np.eye(128, dtype=np.float32),
        "before_in": np.tri(E, k=-1, dtype=np.float32).reshape(1, E, E),
    }
    nc = bacc.Bacc("TRN2", target_bir_lowering=False, num_devices=1)
    maps, args = {}, []
    for name, v in arrays.items():
        v = np.ascontiguousarray(v)
        maps[f"in_{name}"] = v
        args.append(nc.dram_tensor(f"in_{name}", v.shape, mybir.dt.from_np(v.dtype), kind="ExternalInput").ap())
    out = nc.dram_tensor("out_0", a["attn_x"].shape, mybir.dt.float32, kind="ExternalOutput").ap()
    attention_mix_kernel(nc, *args, out)
    r = run(nc, [maps], core_ids=[0])
    return r.results[0]["out_0"]
```

```python
import concourse.bass as bass
from concourse import mybir
from contextlib import ExitStack

FP32 = mybir.dt.float32
BF16 = mybir.dt.bfloat16
ALU = mybir.AluOpType
ACT = mybir.ActivationFunctionType
AX = mybir.AxisListType


def attention_mix_kernel(nc, x, w_attn, w_main, u_t, v_er, s_er, b_qkv, b_o, g_w1, g_b1, g_w2, g_b2,
                         mem_aug, mem_w, ident_in, before_in, out):
    B, S, D = x.shape
    E = g_w2.shape[1]
    GH = g_w1.shape[1]
    HD = 8
    NH = D // HD
    T = S // 128
    J = 4
    HG = NH // J
    RG = 2 * HG
    RU = 2 * RG
    NG = B * RG
    NU = 2 * NG
    HQ = S // 2
    ST = HQ // 128
    GC = J * HD
    MW = D // 2 + 1
    SCALE = float(HD) ** -0.5
    EPS = 1e-5
    PARTS = 3
    TWO_ONES = 1.0 + 0x3F80 / 2 ** 23
    KR = 6 * HD
    Q_RUNS = [(0, 3, 0), (3, 2, 0), (5, 1, 0)]
    K_RUNS = [(0, 3, 0), (3, 2, 1), (5, 1, 2)]
    LOADS = 2 * (len(Q_RUNS) + len(K_RUNS))
    SHIFTS = 8
    JOB = 16 * PARTS

    q_parts = nc.dram_tensor("q_parts", (NG, J, PARTS, HD, S), BF16, kind="Internal").ap()
    k_parts = nc.dram_tensor("k_parts", (NG, J, PARTS, HD, S), BF16, kind="Internal").ap()

    ctx = ExitStack()
    with ctx:
        def sb(name, shape, dt=FP32):
            return ctx.enter_context(nc.sbuf_tensor(name, shape, dt))

        def sem(name):
            return ctx.enter_context(nc.semaphore(name))

        x_all = sb("x_all", [128, B * T, D])
        w_a = sb("w_a", [128, 3, D])
        w_m = sb("w_m", [128, 4, D])
        u_sb = sb("u_sb", [128, 4, D])
        v_sb = sb("v_sb", [128, 4, D])
        s_sb = sb("s_sb", [128, 4])
        bias = sb("bias", [128, 3])
        ob_row = sb("ob_row", [128, D])
        gw1 = sb("gw1", [128, GH])
        gb1 = sb("gb1", [GH, 1])
        gw2 = sb("gw2", [GH, E])
        gb2 = sb("gb2", [1, E])
        mem_sb = sb("mem_sb", [128, 2 * MW])
        mw = sb("mw", [128, 4])
        ident = sb("ident", [128, 128])
        before = sb("before", [1, E, E])

        bn_st = sb("bn_st", [128, B * T, 6])
        bn_mv = sb("bn_mv", [128, B * T, 2])
        rstd = sb("rstd", [128, 3, B * T])
        pass_on = sb("pass_on", [1, 2])
        half_power = sb("half_power", [128, B * T])
        xn = sb("xn", [128, T, D])
        xnt = sb("xnt", [128, S])
        pooled = sb("pooled", [128, 2])
        gate_h = sb("gate_h", [GH, 2 * GH])
        logits = sb("logits", [1, E])
        gate_s = sb("gate_s", [1, 4])
        above = sb("above", [1, E, E])
        ties = sb("ties", [1, E, E])
        rank = sb("rank", [1, E])
        gate_e = sb("gate_e", [1, E])
        gates = sb("gates", [1, E])
        gate_rep = sb("gate_rep", [1, E, 128 // E])
        gs = sb("gs", [128, 4])
        ug = sb("ug", [128, 4, D])
        w_now = sb("w_now", [128, 3, D])
        wo_all = sb("wo_all", [128, B, D])
        full = sb("full", [128, 4, S])
        rest = sb("rest", [128, S])
        part_hi = sb("part_hi", [128, 4, S], BF16)
        part_mid = sb("part_mid", [128, 2, S], BF16)
        part_lo = sb("part_lo", [128, 2, S], BF16)
        elu_a = sb("elu_a", [128, S])
        elu_t = sb("elu_t", [128, S])
        elu_e = sb("elu_e", [128, S])
        a_mem = elu_e[:, :].rearrange("p (t a c) -> p t a c", t=T, a=2)
        mem_inv = sb("mem_inv", [128, 4, ST // 2, 2])
        v_all = sb("v_all", [128, 2 * RG, T, J, HD])

        v_now = sb("v_now", [128, 2, T, J, 32])
        exp_q = sb("exp_q", [128, 2, 2, S], BF16)
        exp_k = sb("exp_k", [128, 2, J, S], BF16)
        max_q = sb("max_q", [128, 2, J, S], BF16)
        max_k = sb("max_k", [128, 2, 2, S], BF16)
        neg_max = sb("neg_max", [128, 2, 16])
        shift_hi = sb("shift_hi", [16, 2, 128], BF16)
        shift_lo = sb("shift_lo", [16, 2, 128], BF16)
        p_exp = sb("p_exp", [128, 2, J, HQ])
        pv_sb = sb("pv_sb", [128, 2, HQ])
        sum_inv = sb("sum_inv", [128, 2, ST, J])
        ctx_all = sb("ctx_all", [128, 2 * RU, ST, GC])

        ctx_b = elu_t[:, :].rearrange("p (t d) -> p t d", t=T)
        ctx_t = xnt
        mixed = sb("mixed", [128, T, D])

        psum = ctx.enter_context(nc.psum_tensor("psum", [128, 8 * 512], FP32))

        def bank(n, k=1):
            return psum[:, n * 512:(n + k) * 512]


        x_first = sem("x_first")
        x_rest = sem("x_rest")
        w_first = sem("w_first")
        w_loaded = sem("w_loaded")
        init_step = sem("init_step")
        init_done = sem("init_done")
        exp_init = sem("exp_init")
        ln_step = sem("ln_step")
        ln_done = sem("ln_done")
        w_scaled = sem("w_scaled")
        pow_in = sem("pow_in")
        pow_out = sem("pow_out")
        xn_ready = sem("xn_ready")
        to_act = sem("to_act")
        act_took = sem("act_took")
        hi_ready = sem("hi_ready")
        hidden_full = sem("hidden_full")
        hidden_ready = sem("hidden_ready")
        logits_full = sem("logits_full")
        gates_ready = sem("gates_ready")
        gates_full = sem("gates_full")
        scale_taken = sem("scale_taken")
        ug_ready = sem("ug_ready")
        weights_full = sem("weights_full")
        weights_ready = sem("weights_ready")
        memory_full = sem("memory_full")
        memory_inv = sem("memory_inv")
        memory_taken = sem("memory_taken")
        gate_step = sem("gate_step")
        gate_exp = sem("gate_exp")
        neg_ready = sem("neg_ready")
        tanh_ready = sem("tanh_ready")
        elu_step = sem("elu_step")
        elu_ready = sem("elu_ready")
        first_step = sem("first_step")
        first_split = sem("first_split")
        split_step = sem("split_step")
        first_stored = [sem("first_q_stored"), sem("first_k_stored")]
        q_stored = sem("q_stored")
        k_stored = sem("k_stored")
        x_step = sem("x_step")
        max_loaded = [sem("max_loaded_even"), sem("max_loaded_odd")]
        exp_loaded = sem("exp_loaded")
        shift_loaded = sem("shift_loaded")
        v_staged = sem("v_staged")
        scores_ready = sem("scores_ready")
        exp_done = sem("exp_done")
        pv_done = sem("pv_done")
        pv_evac = sem("pv_evac")
        ring_full = sem("ring_full")
        ring_free = sem("ring_free")
        maxima_turned = sem("maxima_turned")
        maxima_taken = sem("maxima_taken")
        heads_turned = sem("heads_turned")
        heads_taken = sem("heads_taken")
        hi_done = sem("hi_done")
        inv_done = sem("inv_done")
        ctx_gathered = sem("ctx_gathered")
        ct_ready = sem("ct_ready")
        ct_evac = sem("ct_evac")
        moe_ready = sem("moe_ready")
        mix_ready = sem("mix_ready")
        x_mixed = sem("x_mixed")
        out_summed = sem("out_summed")
        out_stored = sem("out_stored")
        last_stored = sem("last_stored")

        ACT_TAKES = 14
        GATE_STEPS = 12
        TAKE = {"x": 1, "q": 3, "k": 5, "v": 7}

        def take(name, part):
            return TAKE[name] + part % 2 + 6 * (part // 2)

        LEAD = T + T // 2 + 1
        FIRST, LAST = -LEAD, NU * T
        PERIOD = 4 * T
        ROW = RU * T
        LOOP_FROM = T
        ROUNDS = (LAST - LEAD - LOOP_FROM) // PERIOD
        LOOP_TO = LOOP_FROM + ROUNDS * PERIOD
        END = LAST + T // 2
        RR = ROW // PERIOD
        WORK = 2 * PERIOD

        def has_max(s):
            return 0 <= s + LEAD < LAST

        def has_scores(s):
            return 0 <= s < LAST

        def has_pv(s):
            return 0 <= s - 1 < LAST

        def has_shift(s):
            return s % T == 2 * T - LEAD and 0 <= s // T + 1 < NU

        def has_out(s):
            return s % T == 2 and 0 <= s // T - 1 < NU

        entry, entries_before, n = {}, {}, 0
        for s in range(FIRST, END):
            entries_before[s] = n
            for kind in ("max", "max2"):
                if has_max(s):
                    entry[kind, s] = n
                    n += 1
        n_entries = n
        PER_ROUND = entries_before[LOOP_FROM + PERIOD] - entries_before[LOOP_FROM]

        def pv_bank(unit):
            return bank(6 + unit % 2)

        def slot(e):
            return bank(2 + 2 * (e % 2), 2)

        FREE = (LAST - LEAD + 1) * J
        score_bank, emptied_by, last_use = {}, {}, {}
        for n in range(LAST * J):
            score_bank[n] = n % 2 if n < FREE else (n - FREE) % 6
            emptied_by[n] = last_use.get(score_bank[n], -1) + 1
            last_use[score_bank[n]] = n

        def fixed(base, step):
            return base

        TENSOR = {5: ("x", 0), 6: ("x", 1), 7: ("hidden", 0), 9: ("logits", 0), 13: ("q", 0), 14: ("q", 1),
                  15: ("k", 0), 21: ("k", 1), 22: ("v", 0), 23: ("v", 1), 25: ("gates", 0), 29: ("memory", 0),
                  30: ("memory", 1), 31: ("memory", 2), 37: ("memory", 3), 38: ("weights", 0), 39: ("q", 2),
                  45: ("q", 3), 46: ("k", 2), 47: ("k", 3), 53: ("v", 2), 54: ("v", 3), 55: ("turn", 0),
                  61: ("turn", 1), 62: ("out", 0), 63: ("out", 1)}
        TENSOR_0 = {-13: ("hidden", 0), -12: ("logits", 0), -10: ("memory", 0), -9: ("memory", 1),
                    -8: ("memory", 2), -7: ("memory", 3), -5: ("gates", 0), -3: ("weights", 0), -2: ("q", 2),
                    -1: ("q", 3), 0: ("k", 2), 1: ("k", 3), 5: ("v", 2), 6: ("v", 3)}
        VECTOR = {0: [[("norm", 0)], []], 1: [[("norm", 1)], []], 4: [[("norm", 2)], [("norm", 3)]],
                  7: [[("hidden", 0)], []], 9: [[("gate", 1)], [("gate", 2)]], 12: [[("gate", 3)], [("gate", 4)]],
                  13: [[("gate", 5)], [("gate", 6)]], 14: [[("gate", 7)], [("gate", 8)]],
                  15: [[("gate", 9)], [("gate", 10)]], 16: [[("gate", 11)], [("gate", 12)]],
                  17: [[("gate", 13)], []], 22: [[("elu", 0)], []], 23: [[("elu", 1)], []],
                  25: [[("gates", 0)], []], 28: [[("ug", 0), ("ug", 1)], [("ug", 2), ("ug", 3)]],
                  29: [[("memory", 0)], []], 30: [[("memory", 1)], []], 31: [[("memory", 2)], []],
                  37: [[("memory", 3)], []], 38: [[("weights", 0)], []], 48: [[("share", 0)], []],
                  49: [[("share", 1)], []], 51: [[("share", 2)], []], 52: [[("share", 3)], []],
                  62: [[("out", 0)], []], 63: [[("out", 1)], []]}
        VECTOR_0 = {-13: [[("hidden", 0)], []], -12: [[("gate", 1)], [("gate", 2)]],
                    -11: [[("gate", 3)], [("gate", 4)]], -10: [[("memory", 0), ("gate", 5)], [("gate", 6)]],
                    -9: [[("memory", 1), ("gate", 7)], [("gate", 8)]],
                    -8: [[("memory", 2), ("gate", 9)], [("gate", 10)]],
                    -7: [[("memory", 3), ("gate", 11)], [("gate", 12)]], -6: [[("gate", 13)], []],
                    -5: [[("gates", 0)], []], -4: [[("ug", 0), ("ug", 1), ("ug", 2), ("ug", 3)], []],
                    -3: [[("weights", 0)], []]}
        SCALAR = {12: [("gate exp", 0)], 16: [("neg", 0)], 17: [("neg", 1)], 18: [("tanh", 0)],
                  19: [("tanh", 1)], 20: [("exp", 0)], 21: [("exp", 1)], 40: [("gather", 0)],
                  41: [("gather", 1)], 43: [("gather", 2)], 44: [("gather", 3)]}
        SCALAR_0 = {-11: [("gate exp", 0)]}
        OF_OUTPUT = ("turn", "out", "share", "gather")

        def first_row(b):
            return isinstance(b, int) and b == 0

        def wanted(work, b, o):
            return (o if work[0] in OF_OUTPUT else b) is not None

        def tensor_work(m, b, o):
            work = (TENSOR_0 if first_row(b) else TENSOR).get(m)
            return work if work and wanted(work, b, o) else None

        def stream(eng, substep, last):
            def rounds(count, index):
                with eng.Fori(0, count) as i:
                    for s in range(LOOP_FROM, LOOP_FROM + PERIOD):
                        substep(s, lambda base, step: index(i) * step + base, None, None, None)

            def work(b, o, at):
                for m in range(WORK):
                    substep(LOOP_FROM + m, at, m, b, o)

            for s in range(FIRST, LOOP_FROM):
                substep(s, fixed, s, 0, None)
            work(1, None, fixed)
            rounds(RR - 2, lambda i: i + 2)
            with eng.Fori(1, B - 1) as b:
                work(b + 1, b - 1, lambda base, step: b * (RR * step) + base)
                rounds(RR - 2, lambda i: b * RR + i + 2)
            done = (B - 1) * RR
            work(None, B - 2, lambda base, step: base + done * step)
            rounds(ROUNDS - done - 2, lambda i: i + (done + 2))
            for s in range(LOOP_TO, END):
                substep(s, fixed, None, None, None)
            last()

        def load_operand(eng, dst, slot_no, parts, group, runs, done):
            for h in range(2):
                rows = parts[group].rearrange("(p h) c d s -> h (c d) p s", h=2)[h]
                for block, count, part in runs:
                    at = 64 * h + HD * block
                    cols = slice(h, J, 2) if dst.shape[2] == J else slice(0, 2)
                    eng.dma_start(dst[at:at + HD * count, slot_no, cols, :],
                                  rows[HD * part:HD * (part + count)]).then_inc(done, 16)

        def store_parts(eng, k, b, done):
            for c, part in enumerate((part_hi[:, k, :], part_mid[:, k % 2, :], part_lo[:, k % 2, :])):
                dst, at = ((q_parts, c), (k_parts, PARTS - 1 - c))[k % 2]
                first = b * RG + (k // 2) * HG
                groups = slice(first, first + HG) if isinstance(b, int) else bass.ds(first, HG)
                eng.dma_start(dst[groups, :, at, :, :].rearrange("g j d s -> (g j) d s"), part).then_inc(done, 16)

        WEIGHTS = [(w_m[:, :, :], w_main), (u_sb[:, :, :], u_t), (v_sb[:, :, :], v_er), (s_sb[:, :], s_er),
                   (gw1[:, :], g_w1), (gb1[:, :], g_b1), (gw2[:, :], g_w2), (mem_sb[:, :], mem_aug),
                   (before[:, :, :], before_in), (ob_row[:, :], b_o.partition_broadcast(128)),
                   (gb2[:, :], g_b2), (mw[:, 0:1], mem_w.partition_broadcast(128)), (bias[:, :], b_qkv)]

        block = ctx.enter_context(nc.Block())

        @block.sync
        def _(sp):
            for b in range(B):
                sp.dma_start(x_all[:, b * T:(b + 1) * T, :],
                             x[b].rearrange("(t p) d -> p t d", p=128)).then_inc(x_rest if b else x_first, 16)

            for k in range(2):
                sp.wait_ge(first_split, k + 1)
                store_parts(sp, k, 0, first_stored[k])

            sp.wait_ge(init_done, 3)
            sp.wait_ge(first_stored[0], JOB)
            load_operand(sp, max_q, 0, q_parts, 0, Q_RUNS, max_loaded[0])
            sp.wait_ge(first_stored[1], JOB)
            load_operand(sp, max_k, 0, k_parts, 0, K_RUNS, max_loaded[0])
            sp.wait_ge(exp_init, 3)
            load_operand(sp, exp_q, 0, q_parts, 0, Q_RUNS, exp_loaded)
            load_operand(sp, exp_k, 0, k_parts, 0, K_RUNS, exp_loaded)
            load_operand(sp, max_q, 1, q_parts, 1, Q_RUNS, max_loaded[1])
            load_operand(sp, max_k, 1, k_parts, 1, K_RUNS, max_loaded[1])

            def place_shift(unit, g, at):
                sp.wait_ge(maxima_taken, at(unit + 1, 8))
                half = unit % 2
                for c, src in enumerate((shift_hi, shift_lo)):
                    for h in range(2):
                        row = 64 * h + KR + c
                        for p in range(2):
                            first = (2 * h + p) * ST
                            sp.dma_start(exp_q[row:row + 1, g % 2, p, half * HQ:(half + 1) * HQ],
                                         src[first:first + ST, half, :]).then_inc(shift_loaded, 16)

            place_shift(0, 0, fixed)

            def group(g, at):
                if g + 1 < NG:
                    sp.wait_ge(scores_ready, at(8 * T * g + 1, 32 * T))
                    load_operand(sp, exp_q, (g + 1) % 2, q_parts, at(g + 1, 4), Q_RUNS, exp_loaded)
                    load_operand(sp, exp_k, (g + 1) % 2, k_parts, at(g + 1, 4), K_RUNS, exp_loaded)
                place_shift(2 * g + 1, g, at)
                if g + 2 < NG:
                    sp.wait_ge(ring_full, at(entry["max", 2 * T * (g + 1) - LEAD] + 1, 2 * PER_ROUND))
                    if (g + 2) % HG == 0:
                        sp.wait_ge(q_stored, at(JOB * ((g + 2) // HG), JOB))
                        sp.wait_ge(k_stored, at(JOB * ((g + 2) // HG), JOB))
                    load_operand(sp, max_q, g % 2, q_parts, at(g + 2, 4), Q_RUNS, max_loaded[g % 2])
                    load_operand(sp, max_k, g % 2, k_parts, at(g + 2, 4), K_RUNS, max_loaded[g % 2])
                if g + 1 < NG:
                    place_shift(2 * g + 2, g + 1, at)

            group(0, fixed)
            turns = (NG - 3) // HG
            with sp.Fori(0, turns) as i:
                for g in range(1, 1 + HG):
                    group(g, lambda base, step: i * step + base)
            for g in range(1 + turns * HG, NG):
                group(g, fixed)

            for h in range(2):
                sp.wait_ge(out_summed, 2 * (B - 1) + h + 1)
                sp.dma_start(out[B - 1, h * HQ:(h + 1) * HQ].rearrange("(t p) d -> p t d", p=128),
                             mixed[:, h * ST:(h + 1) * ST, :]).then_inc(last_stored, 16)
            sp.wait_ge(last_stored, 32)
            sp.wait_ge(out_stored, 16 * (B - 1))

        @block.gpsimd
        def _(pool):
            pool.memset(half_power[:, :], -0.5).then_inc(init_step, 1)
            pool.wait_ge(init_step, 1)

            def first_root(part, k):
                pool.wait_ge(pow_in, k + 1)
                pool.tensor_tensor(rstd[:, 0, part], rstd[:, 1, part], half_power[:, part],
                                   ALU.pow).then_inc(pow_out, 1)

            first_root(slice(0, T), 0)
            pool.memset(gate_h[:, :], 0.0).then_inc(init_done, 1)
            pool.memset(max_q[:, :, :, :].bitcast(FP32), 0.0).then_inc(init_done, 1)
            pool.memset(max_k[:, :, :, :].bitcast(FP32), 0.0).then_inc(init_done, 1)
            pool.memset(v_now[:, :, :, :, :], 0.0).then_inc(init_step, 1)
            pool.wait_ge(init_step, 2)
            pool.memset(v_now[:, :, :, :, HD:HD + 1], 1.0).then_inc(init_done, 1)
            pool.memset(exp_q[:, :, :, :].bitcast(FP32), 0.0).then_inc(exp_init, 1)
            pool.memset(exp_k[:, :, :, :].bitcast(FP32), 0.0).then_inc(init_step, 1)
            pool.wait_ge(init_step, 3)
            for h in range(2):
                pool.memset(exp_k[64 * h + 32:64 * h + 64, :, h:J:2, :].bitcast(FP32),
                            TWO_ONES).then_inc(exp_init, 1)
                pool.wait_ge(exp_init, 2 + h)
            first_root(slice(T, B * T), 1)

            def split(k, b):
                q_or_k = (q_stored, k_stored)[k % 2]
                pool.wait_ge(hi_ready, b * 4 + (k + 1))
                pool.tensor_tensor(rest[:, :], full[:, k, :], part_hi[:, k, :], ALU.subtract)
                if isinstance(b, int) and b == 0:
                    pool.wait_ge(first_stored[k % 2], JOB)
                else:
                    pool.wait_ge(q_or_k, b * (2 * JOB) + (k // 2 - 1) * JOB)
                pool.tensor_tensor(part_mid[:, k % 2, :], full[:, k, :], part_hi[:, k, :],
                                   ALU.subtract).then_inc(split_step, 1)
                n = 2 * k - 3
                pool.wait_ge(split_step, b * 8 + n)
                pool.tensor_tensor(part_lo[:, k % 2, :], rest[:, :], part_mid[:, k % 2, :],
                                   ALU.subtract).then_inc(split_step, 1)
                pool.wait_ge(split_step, b * 8 + (n + 1))
                pool.tensor_tensor(pass_on[:, 0:1], half_power[0:1, 0:1], half_power[0:1, 0:1], ALU.add)
                store_parts(pool, k, b, q_or_k)

            def add_memory(b):
                am = a_mem.rearrange("p t a c -> p t (a c)")
                pool.wait_ge(memory_taken, b * 4 + 4)
                pool.tensor_tensor(am, am, ob_row[:, :].unsqueeze(1).to_broadcast([128, T, D]),
                                   ALU.add).then_inc(x_step, 1)
                here = x_all[:, bass.ds(b * T, T), :]
                pool.wait_ge(x_step, b * 2 + 1)
                pool.wait_ge(w_loaded, 16 * len(WEIGHTS))
                pool.tensor_tensor(here, here, am, ALU.add).then_inc(x_step, 1)

            def mix(o):
                pool.wait_ge(mix_ready, o + 1)
                pool.wait_ge(x_step, o * 2 + 2)
                pool.wait_ge(w_loaded, 16 * len(WEIGHTS))
                pool.tensor_tensor(mixed[:, :, :], mixed[:, :, :], x_all[:, bass.ds(o * T, T), :],
                                   ALU.add).then_inc(x_mixed, 1)

            def store_out(o):
                pool.wait_ge(out_summed, o * 2 + 2)
                pool.tensor_tensor(pass_on[:, 1:2], half_power[0:1, 0:1], half_power[0:1, 0:1], ALU.add)
                pool.dma_start(out[o].rearrange("(t p) d -> p t d", p=128), mixed[:, :, :]).then_inc(out_stored, 16)

            def substep(s, at, m, b, o):
                if m != (FIRST if first_row(b) else 0):
                    return
                if b is not None:
                    if not first_row(b):
                        split(0, b)
                        split(1, b)
                    add_memory(b)
                    split(2, b)
                if o is not None:
                    mix(o)
                if b is not None:
                    split(3, b)
                if o is not None:
                    store_out(o)

            stream(pool, substep, lambda: mix(B - 1))

        @block.scalar
        def _(act):
            act.dma_start(ident[:, :], ident_in).then_inc(w_first, 16)
            act.dma_start(w_a[:, :, :], w_attn).then_inc(w_first, 16)
            for dst, src in WEIGHTS:
                act.dma_start(dst, src).then_inc(w_loaded, 16)
            act.wait_ge(w_loaded, 16 * len(WEIGHTS))
            nc.scalar.activation(mw[:, 1:2], mw[:, 0:1], ACT.Exp, scale=-1.0).then_inc(gate_exp, 1)

            def empty(name, part, b, src):
                n = take(name, part)
                half = slice((part % 2) * HQ, (part % 2 + 1) * HQ)
                branch = part // 2
                if n == 3 and not first_row(b):
                    act.wait_ge(q_stored, b * (2 * JOB) - JOB)
                    act.wait_ge(k_stored, b * (2 * JOB) - JOB)
                    act.wait_ge(elu_ready, b)
                act.wait_ge(to_act, b * ACT_TAKES + n)
                if name == "x":
                    nc.scalar.activation(xnt[:, half], src, ACT.Identity,
                                         accum_out=pooled[:, part:part + 1]).then_inc(act_took, 1)
                elif name == "v":
                    tiles = slice((part % 2) * ST, (part % 2 + 1) * ST)
                    heads = v_all[:, bass.ds((b % 2) * RG + branch * HG, HG), tiles, :, :].rearrange(
                        "p g t j d -> p t g (j d)")
                    nc.scalar.activation(heads, src.rearrange("p (t g c) -> p t g c", t=ST, g=HG),
                                         ACT.Identity).then_inc(act_took, 1)
                else:
                    k = 2 * branch + (name == "k")
                    off = bias[:, k % 2:k % 2 + 1] if branch else 0.0
                    nc.scalar.activation(full[:, k, half], src, ACT.Identity, bias=off).then_inc(act_took, 1)

            def round_hi(name, part, b):
                k = 2 * (part // 2) + (name == "k")
                half = slice((part % 2) * HQ, (part % 2 + 1) * HQ)
                act.wait_ge(act_took, b * ACT_TAKES + take(name, part))
                done = nc.scalar.activation(part_hi[:, k, half], full[:, k, half], ACT.Identity)
                if part % 2:
                    done.then_inc(hi_ready, 1)

            def prepare(name, part, b, o):
                half = slice(part * HQ, (part + 1) * HQ)
                if name == "gate exp":
                    act.wait_ge(gate_step, b * GATE_STEPS + 2)
                    nc.scalar.activation(gate_e[:, :], logits[:, :], ACT.Exp,
                                         bias=gate_s[:, 0:1]).then_inc(gate_exp, 1)
                elif name == "neg":
                    act.wait_ge(act_took, b * ACT_TAKES + take("q", 1))
                    nc.scalar.activation(elu_a[:, half], full[:, 0, half], ACT.Relu, scale=-1.0).then_inc(neg_ready, 1)
                elif name == "tanh":
                    act.wait_ge(neg_ready, b * 2 + (part + 1))
                    nc.scalar.activation(elu_t[:, half], elu_a[:, half], ACT.Tanh, scale=-0.5)
                elif name == "exp":
                    if not first_row(b):
                        act.wait_ge(x_step, b * 2)
                    nc.scalar.activation(elu_e[:, half], elu_a[:, half], ACT.Exp, scale=-1.0).then_inc(tanh_ready, 1)
                elif name == "gather":
                    gather(part, o)

            def gather(hg, o):
                done = nc.scalar.activation(
                    ctx_b[:, :, hg * GC:(hg + 1) * GC].rearrange("p (h t) c -> p h t c", h=2),
                    ctx_all[:, bass.ds((o % 2) * RU + (RU // 2 + 2 * hg), 2), :, :], ACT.Identity)
                if hg == HG - 1:
                    done.then_inc(ctx_gathered, 1)

            def empty_turned(h, o, src):
                act.wait_ge(ct_ready, o * 2 + (h + 1))
                nc.scalar.activation(ctx_t[:, h * HQ:(h + 1) * HQ], src, ACT.Identity,
                                     bias=bias[:, 2:3]).then_inc(ct_evac, 1)

            def stage_v(g, at):
                nc.scalar.activation(v_now[:, g % 2, :, :, 0:HD], v_all[:, at(g, 2) % (2 * RG), :, :, :],
                                     ACT.Identity).then_inc(v_staged, 1)

            def last():
                o = B - 1
                act.wait_ge(elu_ready, B)
                for hg in range(HG):
                    act.wait_ge(heads_taken, o * RU + RU // 2 + 2 * hg + 2)
                    gather(hg, o)
                for h in range(2):
                    empty_turned(h, o, bank(2 + h))

            def substep(s, at, m, b, o):
                unit = s // T - 1
                work = tensor_work(m, b, o)
                for j in range(J):
                    if has_scores(s):
                        if j == 0 and s >= 2:
                            act.wait_ge(pv_done, at(s - 1, PERIOD))
                        n = J * s + j
                        act.wait_ge(scores_ready, at(n + 1, J * PERIOD))
                        nc.scalar.activation(p_exp[:, s % 2, j, :], bank(score_bank[n]), ACT.Exp,
                                             scale=SCALE).then_inc(exp_done, 1)
                    if j == 1:
                        if s % (2 * T) == 2 and 0 <= s < LAST - 2 * T:
                            stage_v(s // (2 * T) + 1, at)
                        if work and work[0] in TAKE:
                            empty(*work, b, pv_bank(s // T + 1))
                        if work and work[0] == "turn":
                            empty_turned(work[1], o, pv_bank(s // T + 1))
                    if j == 3:
                        if work and work[0] in ("q", "k"):
                            round_hi(*work, b)
                        for name, part in (SCALAR_0 if first_row(b) else SCALAR).get(m, []):
                            if wanted((name, part), b, o):
                                prepare(name, part, b, o)
                if s % T == 0 and 0 <= unit < NU:
                    act.wait_ge(pv_done, at(s, PERIOD))
                    nc.scalar.activation(pv_sb[:, unit % 2, :], bank(6 + unit % 2),
                                         ACT.Identity).then_inc(pv_evac, 1)

            for n, name in enumerate(("x", "q", "k")):
                for h in range(2):
                    empty(name, h, 0, bank(2 + 2 * n + h))
                    if n:
                        round_hi(name, h, 0)
            for name in ("neg", "tanh", "exp"):
                for h in range(2):
                    prepare(name, h, 0, None)
            for h in range(2):
                empty("v", h, 0, bank(h))
            act.wait_ge(act_took, 8)
            act.wait_ge(init_done, 4)
            stage_v(0, fixed)
            stream(act, substep, last)

        @block.tensor
        def _(pe):
            def taken(name, part, b, o):
                if name in TAKE:
                    pe.wait_ge(act_took, b * ACT_TAKES + take(name, part))
                elif name == "hidden":
                    pe.wait_ge(hidden_ready, b + 1)
                elif name == "logits":
                    pe.wait_ge(gate_step, b * GATE_STEPS + 1)
                elif name == "gates":
                    pe.wait_ge(scale_taken, b + 1)
                elif name == "memory":
                    pe.wait_ge(memory_taken, b * 4 + (part + 1))
                elif name == "weights":
                    pe.wait_ge(weights_ready, b + 1)
                elif name == "turn":
                    pe.wait_ge(ct_evac, o * 2 + (part + 1))
                elif name == "out":
                    pe.wait_ge(out_summed, o * 2 + (part + 1))

            def prepare(name, part, b, o, dst):
                h, branch = part % 2, part // 2
                if name == "x":
                    pe.wait_ge(xn_ready, b * 2 + (h + 1))
                    for t in range(ST):
                        last = nc.tensor.transpose(dst[:, t * 128:(t + 1) * 128], xn[:, h * ST + t, :], ident[:, :])
                    last.then_inc(to_act, 1)
                elif name in ("q", "k"):
                    if branch:
                        pe.wait_ge(weights_ready, b + 1)
                    pe.wait_ge(act_took, b * ACT_TAKES + take("x", h))
                    w = (w_now if branch else w_a)[:, int(name == "k"), :]
                    nc.tensor.matmul(dst, w, xnt[:, h * HQ:(h + 1) * HQ], start=True, stop=True).then_inc(to_act, 1)
                elif name == "v":
                    w = (w_now if branch else w_a)[:, 2, :]
                    for t in range(ST):
                        rows = slice((h * ST + t) * 128, (h * ST + t + 1) * 128)
                        last = nc.tensor.matmul(dst[:, t * D:(t + 1) * D], xnt[:, rows], w, start=True, stop=True)
                    last.then_inc(to_act, 1)
                elif name == "hidden":
                    if first_row(b):
                        pe.wait_ge(w_loaded, 16 * len(WEIGHTS))
                        pe.wait_ge(w_scaled, 1)
                    pe.wait_ge(act_took, b * ACT_TAKES + take("x", 1))
                    for half in range(2):
                        last = nc.tensor.matmul(dst[0:GH, 0:1], gw1[:, :], pooled[:, half:half + 1],
                                                start=(half == 0), stop=(half == 1))
                    last.then_inc(hidden_full, 1)
                elif name == "logits":
                    pe.wait_ge(hidden_ready, b + 1)
                    nc.tensor.matmul(dst[0:2 * GH, 128:128 + E], gate_h[:, :], gw2[:, :],
                                     start=True, stop=True).then_inc(logits_full, 1)
                elif name == "gates":
                    pe.wait_ge(gates_ready, b + 1)
                    nc.tensor.matmul(dst[:, 192:193], gate_rep[:, :, :].rearrange("b e r -> b (e r)"),
                                     ident[0:1, 0:1], start=True, stop=True).then_inc(gates_full, 1)
                elif name == "memory":
                    if first_row(b):
                        pe.wait_ge(w_scaled, 5)
                    pe.wait_ge(elu_ready, b + 1)
                    for t in range(2):
                        rows = slice((part * 2 + t) * 128, (part * 2 + t + 1) * 128)
                        last = nc.tensor.matmul(dst[:, 256 * t:256 * t + 2 * MW], elu_a[:, rows], mem_sb[:, :],
                                                start=True, stop=True)
                    last.then_inc(memory_full, 1)
                elif name == "weights":
                    pe.wait_ge(ug_ready, b + 1)
                    for w in range(4):
                        last = nc.tensor.matmul(dst[:, w * D:(w + 1) * D], v_sb[:, w, :], ug[:, w, :],
                                                start=True, stop=True)
                    last.then_inc(weights_full, 1)
                elif name == "turn":
                    pe.wait_ge(ctx_gathered, o + 1)
                    for t in range(ST):
                        last = nc.tensor.transpose(dst[:, t * 128:(t + 1) * 128], ctx_b[:, h * ST + t, :],
                                                   ident[:, :])
                    last.then_inc(ct_ready, 1)
                elif name == "out":
                    pe.wait_ge(ct_evac, o * 2 + (h + 1))
                    for t in range(ST):
                        rows = slice((h * ST + t) * 128, (h * ST + t + 1) * 128)
                        last = nc.tensor.matmul(dst[:, t * 128:(t + 1) * 128], ctx_t[:, rows], wo_all[:, o, :],
                                                start=True, stop=True)
                    last.then_inc(moe_ready, 1)

            def last():
                pe.wait_ge(exp_done, LAST * J)
                for name in ("turn", "out"):
                    for h in range(2):
                        prepare(name, h, None, B - 1, bank((2 if name == "turn" else 4) + h))

            def claim(e, at):
                if e >= 2:
                    pe.wait_ge(ring_free, at(e - 1, PER_ROUND))

            def substep(s, at, m, b, o):
                unit, kt = s // T, s % T

                def before(*places):
                    for place in places:
                        if m is not None and tensor_work(place, b, o):
                            return tensor_work(place, b, o)

                def rest_work():
                    work = tensor_work(m, b, o)
                    if kt >= T // 2 and unit + 1 >= 0 and not before(*range(m - 1, m - 1 - (kt - T // 2), -1)):
                        pe.wait_ge(maxima_taken, at(unit + 2, 4))
                    if kt == 1 and unit >= 1:
                        pe.wait_ge(pv_evac, at(unit, 4))
                    same_unit = before(*range(m - 1, m - kt - 1, -1))
                    if same_unit:
                        taken(*same_unit, b, o)
                    elif first_row(b) and unit < 0:
                        pe.wait_ge(act_took, take("k", 1))
                    prepare(*work, b, o, pv_bank(unit + 1))

                late = kt in (1, T // 2)
                if tensor_work(m, b, o) and not late:
                    rest_work()
                if has_out(s):
                    if before(m - 1 if m is not None else None):
                        taken(*before(m - 1), b, o)
                    pe.wait_ge(pv_evac, at(unit, 4))
                    for t in range(ST):
                        last = nc.tensor.transpose(pv_bank(unit - 1)[:, t * 128:(t + 1) * 128],
                                                   pv_sb[:, (unit - 1) % 2, t * 128:(t + 1) * 128], ident[:, :])
                    last.then_inc(heads_turned, 1)

                def turn_maxima():
                    last_max = entry["max2", (unit + 2) * T - 1 - LEAD]
                    if unit >= 1:
                        pe.wait_ge(heads_taken, at(unit, 4))
                    pe.wait_ge(ring_free, at(last_max + 1, PER_ROUND))
                    nc.tensor.transpose(pv_bank(unit + 1)[0:16, 0:128], neg_max[:, (unit + 1) % 2, :],
                                        ident[:, :]).then_inc(maxima_turned, 1)

                def scores(j):
                    n = J * s + j
                    if emptied_by[n]:
                        pe.wait_ge(exp_done, at(emptied_by[n], J * PERIOD))
                    elif score_bank[n] >= 2:
                        pe.wait_ge(ring_free, n_entries)
                    g, half = unit // 2, unit % 2
                    if kt == 0 and j == 0:
                        if half == 0:
                            pe.wait_ge(exp_loaded, at(16 * LOADS * (g + 1), 32 * LOADS))
                        pe.wait_ge(shift_loaded, at(16 * SHIFTS * (unit + 1), 64 * SHIFTS))
                    nc.tensor.matmul(bank(score_bank[n]), exp_k[:, g % 2, j, kt * 128:(kt + 1) * 128],
                                     exp_q[:, g % 2, j // 2, half * HQ:(half + 1) * HQ],
                                     start=True, stop=True).then_inc(scores_ready, 1)

                def pv():
                    q = s - 1
                    u, t = q // T, q % T
                    pe.wait_ge(exp_done, at(J * s, J * PERIOD))
                    if t == 0 and before(*range(m - 2, m - 2 - T // 2, -1) if m is not None else ()):
                        taken(*before(*range(m - 2, m - 2 - T // 2, -1)), b, o)
                    if t == 0 and u % 2 == 0:
                        pe.wait_ge(v_staged, at(u // 2 + 1, 2))
                    for j in range(J):
                        last = nc.tensor.matmul(bank(6 + u % 2)[32 * j:32 * j + 32, :],
                                                v_now[:, (u // 2) % 2, t, j, :], p_exp[:, q % 2, j, :],
                                                start=(t == 0), stop=(t == T - 1))
                    last.then_inc(pv_done, 1)

                def maxima(h, kind):
                    e = entry[kind, s]
                    mu, mt = (s + LEAD) // T, (s + LEAD) % T
                    mg, half, p, t = mu // 2, mu % 2, mt // ST, mt % ST
                    claim(e, at)
                    if half == 0 and mt == 0 and kind == "max":
                        pe.wait_ge(max_loaded[mg % 2], at(16 * LOADS * (mg // 2 + 1), 16 * LOADS))
                    q0 = half * HQ + t * 128
                    for c in range(2):
                        mm = nc.tensor.matmul(slot(e)[:, c * HQ:(c + 1) * HQ],
                                              max_q[:, mg % 2, 2 * p + h, q0:q0 + 128],
                                              max_k[:, mg % 2, p, c * HQ:(c + 1) * HQ], start=True, stop=True)
                    mm.then_inc(ring_full, 1)

                if has_scores(s):
                    scores(0)
                    scores(1)
                if has_pv(s):
                    pv()
                if tensor_work(m, b, o) and late:
                    rest_work()
                if has_scores(s):
                    scores(2)
                    scores(3)
                if has_max(s):
                    maxima(0, "max")
                if has_shift(s):
                    if before(*range(m, m - kt - 1, -1) if m is not None else ()):
                        taken(*before(*range(m, m - kt - 1, -1)), b, o)
                    turn_maxima()
                if m == WORK - 1 and not first_row(b) and tensor_work(m, b, o):
                    taken(*tensor_work(m, b, o), b, o)
                if has_max(s):
                    maxima(1, "max2")

            pe.wait_ge(w_first, 32)
            for n, name in enumerate(("x", "q", "k", "v")):
                for h in range(2):
                    prepare(name, h, 0, None, bank((2 + 2 * n + h) % 8))
            pe.wait_ge(act_took, 8)
            stream(pe, substep, last)

        @block.vector
        def _(dve):
            def variance(part, k):
                for t in range(part.start, part.stop):
                    last = nc.vector.bn_stats(bn_st[:, t, :], x_all[:, t, :])
                last.then_inc(ln_step, 1)
                dve.wait_ge(ln_step, 5 * k + 1)
                for t in range(part.start, part.stop):
                    last = nc.vector.bn_aggr(bn_mv[:, t, :], bn_st[:, t, :])
                last.then_inc(ln_step, 1)
                dve.wait_ge(ln_step, 5 * k + 2)
                nc.vector.tensor_scalar(rstd[:, 1, part], bn_mv[:, part, 1], EPS, None, ALU.add).then_inc(pow_in, 1)

            def inverse_root(part, k):
                first, var, tmp = (rstd[:, i, part] for i in range(3))
                dve.wait_ge(pow_out, k + 1)
                nc.vector.tensor_tensor(tmp, first, first, ALU.mult).then_inc(ln_step, 1)
                dve.wait_ge(ln_step, 5 * k + 3)
                nc.vector.tensor_tensor(tmp, tmp, var, ALU.mult).then_inc(ln_step, 1)
                dve.wait_ge(ln_step, 5 * k + 4)
                nc.vector.tensor_scalar(tmp, tmp, -0.5, 1.5, ALU.mult, ALU.add).then_inc(ln_step, 1)
                dve.wait_ge(ln_step, 5 * k + 5)
                nc.vector.tensor_tensor(first, first, tmp, ALU.mult).then_inc(ln_done, 1)
                dve.wait_ge(ln_done, k + 1)

            def normalise(j, b):
                for t in (2 * j, 2 * j + 1):
                    last = nc.vector.tensor_scalar(xn[:, t, :], x_all[:, b * T + t, :], bn_mv[:, b * T + t, 0:1],
                                                   rstd[:, 0, bass.ds(b * T + t, 1)], ALU.subtract, ALU.mult)
                if j % 2:
                    last.then_inc(xn_ready, 1)

            dve.wait_ge(x_first, 16)
            variance(slice(0, T), 0)
            inverse_root(slice(0, T), 0)
            for j in range(T // 2):
                normalise(j, 0)
            first_rest = mixed[:, :, :].rearrange("p t d -> p (t d)")
            for k in range(2):
                dve.wait_ge(hi_ready, k + 1)
                if k:
                    dve.wait_ge(first_split, 1)
                nc.vector.tensor_tensor(first_rest, full[:, k, :], part_hi[:, k, :],
                                        ALU.subtract).then_inc(first_step, 1)
                dve.wait_ge(first_step, 2 * k + 1)
                nc.vector.tensor_copy(part_mid[:, k, :], first_rest).then_inc(first_step, 1)
                dve.wait_ge(first_step, 2 * k + 2)
                nc.vector.tensor_tensor(part_lo[:, k, :], first_rest, part_mid[:, k, :],
                                        ALU.subtract).then_inc(first_split, 1)
            dve.wait_ge(x_rest, 16 * (B - 1))
            variance(slice(T, B * T), 1)
            dve.wait_ge(w_loaded, 16 * len(WEIGHTS))
            nc.vector.tensor_scalar(gw1[:, :], gw1[:, :], 1.0 / S, None, ALU.mult).then_inc(w_scaled, 1)
            dve.wait_ge(gate_exp, 1)
            nc.vector.tensor_scalar(mw[:, 1:2], mw[:, 1:2], 1.0, None, ALU.add).then_inc(w_scaled, 1)
            dve.wait_ge(w_scaled, 2)
            nc.vector.reciprocal(mw[:, 2:3], mw[:, 1:2]).then_inc(w_scaled, 1)
            dve.wait_ge(w_scaled, 3)
            nc.vector.tensor_scalar(mw[:, 3:4], mw[:, 2:3], -1.0, 1.0, ALU.mult, ALU.add).then_inc(w_scaled, 1)
            dve.wait_ge(w_scaled, 4)
            weighted = mem_sb[:, :].rearrange("p (a c) -> p a c", a=2)[:, :, 0:MW - 1]
            nc.vector.tensor_scalar(weighted, weighted, mw[:, 2:3], None, ALU.mult).then_inc(w_scaled, 1)

            def gate(i, b):
                if i == 1:
                    dve.wait_ge(logits_full, b + 1)
                    step = nc.vector.tensor_tensor(logits[:, :], pv_bank(gate_bank(b))[0:1, 128:128 + E], gb2[:, :],
                                                   ALU.add)
                else:
                    dve.wait_ge(gate_step, b * GATE_STEPS + (i - 1))
                other = logits[:, :].unsqueeze(1).to_broadcast([1, E, E])
                own = logits[:, :].unsqueeze(2).to_broadcast([1, E, E])
                if i == 2:
                    step = nc.vector.tensor_reduce(gate_s[:, 0:1], logits[:, :], AX.X, ALU.max, negate=True)
                elif i == 3:
                    step = nc.vector.tensor_tensor(above[:, :, :], other, own, ALU.is_gt)
                elif i == 4:
                    step = nc.vector.tensor_tensor(ties[:, :, :], other, own, ALU.is_equal)
                elif i == 5:
                    step = nc.vector.tensor_tensor(ties[:, :, :], ties[:, :, :], before[:, :, :], ALU.mult)
                elif i == 6:
                    step = nc.vector.tensor_tensor(above[:, :, :], above[:, :, :], ties[:, :, :], ALU.add)
                elif i == 7:
                    step = nc.vector.tensor_reduce(rank[:, :], above[:, :, :], AX.X, ALU.add)
                elif i == 8:
                    step = nc.vector.tensor_scalar(rank[:, :], rank[:, :], 2.0, None, ALU.is_lt)
                elif i == 9:
                    dve.wait_ge(gate_exp, b + 2)
                    step = nc.vector.tensor_tensor(gates[:, :], gate_e[:, :], rank[:, :], ALU.mult)
                elif i == 10:
                    step = nc.vector.tensor_reduce(gate_s[:, 1:2], gates[:, :], AX.X, ALU.add)
                elif i == 11:
                    step = nc.vector.reciprocal(gate_s[:, 2:3], gate_s[:, 1:2])
                elif i == 12:
                    step = nc.vector.tensor_scalar(gates[:, :], gates[:, :], gate_s[:, 2:3], None, ALU.mult)
                elif i == 13:
                    nc.vector.tensor_copy(gate_rep[:, :, :], gates[:, :].unsqueeze(2).to_broadcast(
                        [1, E, 128 // E])).then_inc(gates_ready, 1)
                if i <= GATE_STEPS:
                    step.then_inc(gate_step, 1)

            def gate_bank(b):
                return (-12 if first_row(b) else LOOP_FROM + 9) // T + 1

            def prepare(name, part, b, o, src):
                if name == "norm":
                    normalise(part, b)
                elif name == "hidden":
                    if first_row(b):
                        dve.wait_ge(init_done, 4)
                    dve.wait_ge(hidden_full, b + 1)
                    nc.vector.tensor_scalar(gate_h[:, 0:1], src[0:GH, 0:1], gb1[:, 0:1], 0.0, ALU.add,
                                            ALU.max).then_inc(hidden_ready, 1)
                elif name == "gate":
                    gate(part, b)
                elif name == "gates":
                    dve.wait_ge(gates_full, b + 1)
                    nc.vector.tensor_scalar(gs[:, :], s_sb[:, :], src[:, 192:193], None,
                                            ALU.mult).then_inc(scale_taken, 1)
                elif name == "ug":
                    if part == 0:
                        dve.wait_ge(scale_taken, b + 1)
                    last = nc.vector.tensor_scalar(ug[:, part, :], u_sb[:, part, :], gs[:, part:part + 1], None,
                                                   ALU.mult)
                    if part == 3:
                        last.then_inc(ug_ready, 1)
                elif name == "elu" and part == 0:
                    dve.wait_ge(tanh_ready, b * 2 + 2)
                    nc.vector.scalar_tensor_tensor(elu_t[:, :], elu_e[:, :], 1.0, elu_t[:, :], ALU.add,
                                                   ALU.mult).then_inc(elu_step, 1)
                elif name == "elu":
                    dve.wait_ge(elu_step, b + 1)
                    nc.vector.scalar_tensor_tensor(elu_a[:, :], full[:, 0, :], 0.0, elu_t[:, :], ALU.max,
                                                   ALU.add).then_inc(elu_ready, 1)
                elif name == "memory":
                    num = src.rearrange("p (t n) -> p t n", t=2)[:, :, 0:2 * MW].rearrange(
                        "p t (a c) -> p t a c", a=2)
                    dve.wait_ge(memory_full, b * 4 + (part + 1))
                    nc.vector.reciprocal(mem_inv[:, part, :, :], num[:, :, :, MW - 1]).then_inc(memory_inv, 1)
                    dve.wait_ge(memory_inv, b * 4 + (part + 1))
                    nc.vector.tensor_tensor(a_mem[:, part * 2:(part + 1) * 2, :, :], num[:, :, :, 0:MW - 1],
                                            mem_inv[:, part, :, :].unsqueeze(3).to_broadcast([128, 2, 2, MW - 1]),
                                            ALU.mult).then_inc(memory_taken, 1)
                elif name == "weights":
                    dve.wait_ge(weights_full, b + 1)
                    nc.vector.tensor_tensor(wo_all[:, b, :], src[:, 3 * D:4 * D], w_m[:, 3, :], ALU.add)
                    nc.vector.tensor_tensor(w_now[:, :, :], src[:, 0:3 * D].rearrange("p (w o) -> p w o", w=3),
                                            w_m[:, 0:3, :], ALU.add).then_inc(weights_ready, 1)
                elif name == "share":
                    if part == 0 and not first_row(o):
                        dve.wait_ge(out_stored, o * 16)
                    last = nc.vector.tensor_scalar(
                        mixed[:, :, part * GC:(part + 1) * GC].rearrange("p (h t) c -> p h t c", h=2),
                        ctx_all[:, bass.ds((o % 2) * RU + 2 * part, 2), :, :], mw[:, 3:4], None, ALU.mult)
                    if part == HG - 1:
                        last.then_inc(mix_ready, 1)
                elif name == "out":
                    dve.wait_ge(x_mixed, o + 1)
                    dve.wait_ge(moe_ready, o * 2 + (part + 1))
                    rows = mixed[:, part * ST:(part + 1) * ST, :]
                    nc.vector.tensor_tensor(rows, src.rearrange("p (t d) -> p t d", t=ST), rows,
                                            ALU.add).then_inc(out_summed, 1)

            def last():
                for h in range(2):
                    prepare("out", h, None, B - 1, bank(4 + h))

            def substep(s, at, m, b, o):
                unit = s // T

                def work(point):
                    places = VECTOR_0 if first_row(b) else VECTOR
                    for name, part in places.get(m, ((), ()))[point]:
                        if wanted((name, part), b, o):
                            prepare(name, part, b, o, pv_bank(unit + 1))
                    if s == LAST - T // 2 and point == 0:
                        for part in range(HG):
                            prepare("share", part, None, B - 1, None)

                turned = pv_bank(unit + 1)[0:16, 0:128]
                if has_shift(s - 1):
                    dve.wait_ge(hi_done, at(unit + 2, 4))
                    nc.vector.tensor_tensor(shift_lo[:, (unit + 1) % 2, :], turned, shift_hi[:, (unit + 1) % 2, :],
                                            ALU.subtract).then_inc(maxima_taken, 1)
                work(0)
                def maximum(h, kind):
                    e = entry[kind, s]
                    mu, mt = (s + LEAD) // T, (s + LEAD) % T
                    col = 8 * h + mt
                    dve.wait_ge(ring_full, at(e + 1, PER_ROUND))
                    nc.vector.tensor_reduce(neg_max[:, mu % 2, col:col + 1], slot(e), AX.X, ALU.max,
                                            negate=True).then_inc(ring_free, 1)

                if has_out(s):
                    heads = pv_bank(unit - 1).rearrange("p (t j c) -> p t j c", t=ST, j=J)
                    dve.wait_ge(heads_turned, at(unit, 4))
                    nc.vector.reciprocal(sum_inv[:, (unit - 1) % 2, :, :], heads[:, :, :, HD]).then_inc(inv_done, 1)
                if has_max(s):
                    maximum(0, "max")
                if has_out(s):
                    dve.wait_ge(inv_done, at(unit, 4))
                    nc.vector.tensor_tensor(
                        ctx_all[:, at(unit - 1, 4) % (2 * RU), :, :].rearrange("p t (j d) -> p t j d", j=J),
                        heads[:, :, :, 0:HD],
                        sum_inv[:, (unit - 1) % 2, :, :].unsqueeze(3).to_broadcast([128, ST, J, HD]),
                        ALU.mult).then_inc(heads_taken, 1)
                work(1)
                if has_shift(s):
                    dve.wait_ge(maxima_turned, at(unit + 2, 4))
                    if unit >= 1:
                        dve.wait_ge(shift_loaded, at(16 * SHIFTS * unit, 64 * SHIFTS))
                    nc.vector.tensor_copy(shift_hi[:, (unit + 1) % 2, :], turned).then_inc(hi_done, 1)
                if has_max(s):
                    maximum(1, "max2")

            prepare("elu", 0, 0, None, None)
            prepare("elu", 1, 0, None, None)
            inverse_root(slice(T, B * T), 1)
            stream(dve, substep, last)


def kernel(**inputs):
    import numpy as np
    import concourse.bacc as bacc
    from concourse.bass_utils import run_bass_kernel_spmd as run

    a = {k.replace("L0_", ""): np.ascontiguousarray(v) for k, v in inputs.items()}
    ws = ("q", "k", "v", "o")
    E, D, R = a["ffn_qU"].shape
    kv = a["attn_Wk"].shape[1]
    hd = 8

    def twice(w):
        return np.repeat(w.reshape(D, kv // hd, hd), 2, axis=1).reshape(D, D)

    mem = np.zeros((D, 2 * (kv + 1)), np.float32)
    for i in range(2):
        mem[i * kv:(i + 1) * kv, i * (kv + 1):i * (kv + 1) + kv] = a["attn_memory"]
        mem[i * kv:(i + 1) * kv, i * (kv + 1) + kv] = a["attn_memory_norm"]
    arrays = {
        "x": a["attn_x"],
        "w_attn": np.stack([a["attn_Wq"], twice(a["attn_Wk"]), twice(a["attn_Wv"])], axis=1),
        "w_main": np.stack([a[f"ffn_{w}Wm"].T for w in ws], axis=1),
        "u_t": np.stack([a[f"ffn_{w}U"].transpose(0, 2, 1).reshape(E * R, D) for w in ws], axis=1),
        "v_er": np.stack([a[f"ffn_{w}V"].reshape(E * R, D) for w in ws], axis=1),
        "s_er": np.stack([a[f"ffn_{w}S"].reshape(E * R) for w in ws], axis=1),
        "b_qkv": np.stack([a[f"ffn_{w}b"] for w in ("q", "k", "v")], axis=1),
        "b_o": a["ffn_ob"],
        "g_w1": a["ffn_gw1"].T,
        "g_b1": a["ffn_gb1"].reshape(-1, 1),
        "g_w2": a["ffn_gw2"].T,
        "g_b2": a["ffn_gb2"].reshape(1, E),
        "mem_aug": mem,
        "mem_w": a["attn_memory_weight"],
        "ident_in": np.eye(128, dtype=np.float32),
        "before_in": np.tri(E, k=-1, dtype=np.float32).reshape(1, E, E),
    }
    nc = bacc.Bacc("TRN2", target_bir_lowering=False, num_devices=1)
    maps, args = {}, []
    for name, v in arrays.items():
        v = np.ascontiguousarray(v)
        maps[f"in_{name}"] = v
        args.append(nc.dram_tensor(f"in_{name}", v.shape, mybir.dt.from_np(v.dtype), kind="ExternalInput").ap())
    out = nc.dram_tensor("out_0", a["attn_x"].shape, mybir.dt.float32, kind="ExternalOutput").ap()
    attention_mix_kernel(nc, *args, out)
    r = run(nc, [maps], core_ids=[0])
    return r.results[0]["out_0"]
```
